# Optimizing a Trainium2 kernel written in Bass

```python
import numpy as np
import jax
import jax.numpy as jnp

def _softmax(x, axis=-1):
    return jax.nn.softmax(x, axis=axis)

def _gelu(x):
    return jax.nn.gelu(x, approximate=True)

def _silu(x):
    return jax.nn.silu(x)

def _sigmoid(x):
    return jax.nn.sigmoid(x)

def _layernorm(x, axis=-1, eps=1e-05):
    m = jnp.mean(x, axis=axis, keepdims=True)
    v = jnp.var(x, axis=axis, keepdims=True)
    return (x - m) / jnp.sqrt(v + eps)

def _scatter_add(tgt, idx, src, axis=0):
    return tgt.at[idx].add(src)

def _segment_sum(src, seg, n):
    return jax.ops.segment_sum(src, seg, n)
kernel_name = 'mk_gnn_ffn_d1_gnn_r8_db353d'

def setup_inputs(seed: int=0):
    np.random.seed(seed)
    _w = jnp.asarray

    def _rec_inputs():
        import jax
        import jax.numpy as jnp
        _gk = jax.random.key(seed)
        x = -0.0002117 + 1 * jax.random.normal(jax.random.fold_in(_gk, 1), (12500, 256), jnp.float32)
        _s = jax.random.randint(jax.random.fold_in(_gk, 2), (100000,), 0, 12500, jnp.int32)
        _d = jax.random.randint(jax.random.fold_in(_gk, 3), (100000,), 0, 12500, jnp.int32)
        _loop = jnp.arange(12500, dtype=jnp.int32)
        src = jnp.concatenate([_s, _d, _loop])
        dst = jnp.concatenate([_d, _s, _loop])
        _o = jnp.argsort(dst, stable=True)
        src = src[_o]
        dst = dst[_o]
        edge_weight = jax.random.uniform(jax.random.fold_in(_gk, 12), (212500,), jnp.float32, 0.0, 1)
        return (x, src, dst, edge_weight)
    x, src, dst, edge_weight = _rec_inputs()

    def _L0_gnn_setup():
        import jax, jax.numpy as jnp
        import numpy as np
        N_NODES = 12500
        key = jax.random.key(seed)
        k1, k2, k3, k4, k5, k6 = jax.random.split(key, 6)
        n, e, d_in, d_out = (N_NODES, 200000, 256, 256)
        features = jax.random.normal(k1, (n, d_in), dtype=jnp.float32)
        edge_src = jax.random.randint(k2, (e,), 0, n, dtype=jnp.int32)
        edge_dst = jax.random.randint(k3, (e,), 0, n, dtype=jnp.int32)
        edge_weight = jax.random.uniform(k4, (e,), dtype=jnp.float32)
        a = 1.0 / np.sqrt(d_out)
        W = jax.random.uniform(k5, (d_out, d_in), dtype=jnp.float32, minval=-a, maxval=a)
        b = jax.random.uniform(k6, (d_out,), dtype=jnp.float32, minval=-a, maxval=a)
        return {'features': features, 'edge_src': edge_src, 'edge_dst': edge_dst, 'edge_weight': edge_weight, 'W': W, 'b': b}
    _L0_gnn_all = _L0_gnn_setup()
    _L0_gnn_in = {k: v for k, v in _L0_gnn_all.items() if k in ('W', 'b')}
    del _L0_gnn_all

    def _L0_ffn_setup():
        import math
        import jax, jax.numpy as jnp
        import numpy as np
        CAPACITY_FACTOR = 1.25
        key = jax.random.key(seed)
        ks = jax.random.split(key, 5)
        B, L, D, F, E = (8, 1024, 256, 1024, 8)
        h = jax.random.normal(ks[0], (B, L, D), dtype=jnp.float32)
        gate_w = jax.random.normal(ks[1], (D, E), dtype=jnp.float32) * 0.02
        gate_b = jnp.zeros((E,), dtype=jnp.float32)
        w1 = jax.random.normal(ks[2], (E, D, F), dtype=jnp.float32) * (1.0 / math.sqrt(D))
        b1 = jnp.zeros((E, F), dtype=jnp.float32)
        w2 = jax.random.normal(ks[3], (E, F, D), dtype=jnp.float32) * (1.0 / math.sqrt(F))
        b2 = jnp.zeros((E, D), dtype=jnp.float32)
        return {'h': h, 'gate_w': gate_w, 'gate_b': gate_b, 'w1': w1, 'b1': b1, 'w2': w2, 'b2': b2}
    _L0_ffn_all = _L0_ffn_setup()
    _L0_ffn_in = {k: v for k, v in _L0_ffn_all.items() if k in ('gate_w', 'gate_b', 'w1', 'b1', 'w2', 'b2')}
    del _L0_ffn_all
    return {'x': x, 'src': src, 'dst': dst, 'edge_weight': edge_weight, 'L0_gnn_W': _L0_gnn_in['W'], 'L0_gnn_b': _L0_gnn_in['b'], 'L0_ffn_gate_w': _L0_ffn_in['gate_w'], 'L0_ffn_gate_b': _L0_ffn_in['gate_b'], 'L0_ffn_w1': _L0_ffn_in['w1'], 'L0_ffn_b1': _L0_ffn_in['b1'], 'L0_ffn_w2': _L0_ffn_in['w2'], 'L0_ffn_b2': _L0_ffn_in['b2']}

def reference(x, src, dst, edge_weight, L0_gnn_W, L0_gnn_b, L0_ffn_gate_w, L0_ffn_gate_b, L0_ffn_w1, L0_ffn_b1, L0_ffn_w2, L0_ffn_b2):
    import jax
    import jax.numpy as jnp

    def _L0_gnn_ref(features, edge_src, edge_dst, edge_weight, W, b):
        import jax, jax.numpy as jnp
        import numpy as np
        N_NODES = 12500
        msgs = features[edge_src] * edge_weight[:, None]
        agg = jax.ops.segment_sum(msgs, edge_dst, num_segments=N_NODES)
        return agg @ W.T + b

    def _L0_ffn_ref(h, gate_w, gate_b, w1, b1, w2, b2):
        import math
        import jax, jax.numpy as jnp
        import numpy as np
        CAPACITY_FACTOR = 1.25
        B, L, D = h.shape
        E = gate_w.shape[1]
        T = B * L
        C = max(1, math.ceil(CAPACITY_FACTOR * T / E))
        x = h.reshape(T, D)
        logits = x @ gate_w + gate_b
        probs = jax.nn.softmax(logits, axis=-1)
        idx = jnp.argmax(probs, axis=-1)
        prb = jnp.take_along_axis(probs, idx[:, None], axis=1)[:, 0]
        one_hot = jax.nn.one_hot(idx, E, dtype=jnp.float32)
        pos = (jnp.cumsum(one_hot, axis=0) * one_hot).sum(-1).astype(jnp.int32) - 1
        kept = pos < C
        pos_safe = jnp.where(kept, pos, C)
        buf = jnp.zeros((E, C, D), dtype=h.dtype).at[idx, pos_safe].set(x, mode='drop')
        hmid = jax.nn.relu(jnp.einsum('ecd,edf->ecf', buf, w1) + b1[:, None, :])
        ybuf = jnp.einsum('ecf,efd->ecd', hmid, w2) + b2[:, None, :]
        pos_g = jnp.minimum(pos, C - 1)
        y_tok = ybuf[idx, pos_g] * (prb * kept)[:, None]
        y = y_tok.reshape(B, L, D)
        y = jnp.nan_to_num(y, nan=0.0, posinf=10000.0, neginf=-10000.0)
        return y
    x = x + _L0_gnn_ref(_layernorm(x, axis=-1), src, dst, edge_weight, L0_gnn_W, L0_gnn_b)
    x = x + _L0_ffn_ref(_layernorm(x, axis=-1)[None], L0_ffn_gate_w, L0_ffn_gate_b, L0_ffn_w1, L0_ffn_b1, L0_ffn_w2, L0_ffn_b2)[0]
    return x

_drawn_inputs = setup_inputs


def setup_inputs(seed=0):
    import zlib

    import numpy as np

    out = dict(_drawn_inputs(seed))
    spreads = {'L0_ffn_gate_b': (0.0, 0.1), 'L0_ffn_b1': (0.0, 0.8), 'L0_ffn_b2': (0.0, 0.724)}
    factors = {}
    for name, (base, spread) in spreads.items():
        noise = np.random.default_rng([zlib.crc32(name.encode()), seed]).standard_normal(out[name].shape)
        drawn = base * np.exp(spread * noise) if base else spread * noise
        out[name] = jnp.asarray(drawn.astype(out[name].dtype))
    for name, factor in factors.items():
        out[name] = (out[name] * factor).astype(out[name].dtype)
    return out
```

```python
from contextlib import ExitStack, contextmanager

import concourse.bass as bass
from concourse import mybir

P = 128
ALU = mybir.AluOpType
ACT = mybir.ActivationFunctionType
F32 = mybir.dt.float32
I32 = mybir.dt.int32
AX_X = mybir.AxisListType.X

WIN = 64
LAG = 2
CAPACITY_FACTOR = 1.25
EPS = 1e-5
FLT_MAX = 3.4028234663852886e38
LN_TILES = 7
LN_BUFS = 4
C_IDENT, C_TRI, C_IOTA, C_RANK, C_SEG = 0, 128, 256, 320, 328


def segments_of(tiles):
    if tiles >= 90:
        last = [27, 19, 13]
        return [tiles - sum(last)] + last
    half = tiles // 2
    return [half - 1 + half % 2, tiles - (half - 1 + half % 2)]


def capacity_of(tokens, experts):
    return max(1, -int(-CAPACITY_FACTOR * tokens // experts))


def layout_of(n, e, experts):
    tiles = -(-n // P)
    edge_tiles = -(-e // P)
    group = -(-edge_tiles // tiles)
    third = -(-group // 3)
    subs = [third, third, group - 2 * third]
    seg = segments_of(tiles)
    caps = [P * (t + 1) for t in seg]
    base = [0]
    for c in caps:
        base.append(base[-1] + (experts + 1) * c)
    return dict(tiles=tiles, group=group, subs=subs, seg=seg, caps=caps, base=base,
                columns=(tiles + 1) * group, ffn=[t + experts - 1 for t in seg])


def buffer_of(s, last):
    return 2 if s == last else min(s, 1)


def timeline_of(tiles, seg, ffn):
    steps = [dict(agg=0), dict(agg=1)]
    node = k = f = 0
    last = len(seg) - 1
    ends = [seg[0], sum(seg[:last]), tiles]
    todo = 0

    def fins(it, most, ready):
        nonlocal f
        which = next(g for g in range(3) if f < ends[g]) if f < tiles else 2
        n = min(most, ends[which] - f)
        if n > 0 and f + n <= ready:
            it.update(fin=f, fins=n, source=which)
            f += n

    for s, t in enumerate(seg):
        for j in range(t):
            it = dict(node=node)
            if node + LAG < tiles:
                it["agg"] = node + LAG
            if todo and j >= 1:
                it.update(ffn=k, to=buffer_of(s - 1, last))
                k += 2
                todo -= 2
                if s == 2:
                    fins(it, 2, ends[0])
            steps.append(it)
            node += 1
        while todo:
            steps.append(dict(ffn=k, to=buffer_of(s - 1, last)))
            k += 2
            todo -= 2
        steps.append(dict(sched=s))
        todo = ffn[s]
    while todo:
        it = dict(ffn=k, to=2)
        fins(it, 6, ends[1])
        k += 2
        todo -= 2
        steps.append(it)
    steps.append(dict(sched=len(seg)))
    while f < tiles:
        it = {}
        fins(it, 2, tiles)
        steps.append(it)

    def alone(it):
        return ("sched" in it or it.get("agg") == 0 or it.get("node") in (0, tiles - 1) or it.get("ffn") == 0
                or it.get("fin") == 0 or ("fin" in it and it["fin"] + it["fins"] == tiles))

    out = []
    for it in steps:
        if out and not alone(it) and not alone(out[-1][1]):
            count, first = out[-1]
            stride = dict(agg=1, node=1, ffn=2, fin=first.get("fins"))
            if first.keys() == it.keys() and first.get("fins") == it.get("fins") and all(
                    it[x] == first[x] + count * stride.get(x, 0) for x in it if x != "fins"):
                out[-1] = (count + 1, first)
                continue
        out.append((1, it))
    return out


def gnn_moe_kernel(nc, x, src_t, dst_t, w_t, w_gnn, b_gnn, gate_w, gate_b, w1, b1, w2, b2, consts, limits,
                   zeros, out, sizes):
    N, D = x.shape
    E8 = gate_w.shape[2]
    F = b1.shape[1] * b1.shape[2]
    FC = F // P
    KD = D // P
    HALF = FC // 2
    NT, G, SUBS, SEG, CAPS, BASE, COLS, FFN = (sizes[q] for q in (
        "tiles", "group", "subs", "seg", "caps", "base", "columns", "ffn"))
    OFF = [0, SUBS[0], SUBS[0] + SUBS[1]]
    NG = NT
    LAST_ROWS = N - (NT - 1) * P
    CAP = capacity_of(N, E8)
    NC = -(-(N + WIN) // WIN) * WIN
    WINDOWS = NC // WIN
    S = len(SEG)
    KTOT = sum(FFN)
    ROWS = BASE[-1]
    TIMELINE = timeline_of(NT, SEG, FFN)
    LN_ROWS = P * LN_TILES
    LN_FULL = N // LN_ROWS
    assert D == 2 * P and E8 == 8 and min(SEG) >= 7 and max(FFN) <= WIN and LAST_ROWS > 0

    ln_dram = nc.dram_tensor("normed", (N, D), F32).ap()
    x2_dram = nc.dram_tensor("x_after_gnn", (N, D), F32).ap()
    hbuf = nc.dram_tensor("rows_by_expert", (ROWS, D), F32).ap()
    KBUF = [0, FFN[0], sum(FFN[:-1]), KTOT]
    ybuf = [nc.dram_tensor(f"expert_outputs{g}", (max(KBUF[g + 1] - KBUF[g], 1) * P, D), F32).ap() for g in range(3)]

    with ExitStack() as ctx:
        def sb(name, shape, dt=F32):
            return ctx.enter_context(nc.sbuf_tensor(name, shape, dt))

        def psum(name, shape):
            return ctx.enter_context(nc.psum_tensor(name, shape, F32))

        def sem(name):
            return ctx.enter_context(nc.semaphore(name))

        aggT = sb("aggT", [P, KD, NC])
        src_sb = sb("src_sb", [P, COLS], I32)
        rel = sb("rel", [P, COLS])
        wgt = sb("wgt", [P, COLS])
        base_bc = sb("base_bc", [P, 3 * (NG + 1)])
        base_i = sb("base_i", [1, 3 * (NG + 1)], I32)
        msg = sb("msg", [P, G, D])
        onehot = sb("onehot", [P, G, WIN])
        idx = sb("idx", [P, G], I32)
        cst = sb("cst", [P, C_SEG + E8 * S])
        ones = sb("ones", [P, P])
        eps = sb("eps", [P, 1])
        wg_sb = sb("wg_sb", [P, KD, D])
        bg_sb = sb("bg_sb", [1, D])
        gw_sb = sb("gw_sb", [P, KD, E8])
        gb_sb = sb("gb_sb", [P, E8])
        aggS = sb("aggS", [P, KD, P])
        xt = sb("xt", [P, D])
        hrow = sb("hrow", [P, D])
        hTs = sb("hTs", [P, KD, P])
        st6 = sb("st6", [P, 6])
        mv = sb("mv", [P, 2])
        sd = sb("sd", [P, 1])
        rs = sb("rs", [P, 1])
        rt = sb("rt", [P, 8 * E8])
        sc = sb("sc", [P, 8])
        slot_i = sb("slot_i", [P, 1], I32)
        slots = sb("slots", [P, NT])
        chosen = sb("chosen", [P, NT])
        gain = sb("gain", [P, NT])
        seen = sb("seen", [P, E8])
        offs = sb("offs", [P, E8])
        WSZ = KD * F + FC * D + FC + D
        wsl = sb("wsl", [P, 2, WSZ])
        hin = sb("hin", [P, 2, D])
        hTf = sb("hTf", [P, KD, P])
        hmid = sb("hmid", [P, FC, P])
        yrow = sb("yrow", [P, 2, D])
        plan = sb("plan", [1, 4 * KTOT], I32)
        pads = sb("pads", [1, E8 * S], I32)
        yg = sb("yg", [P, 2, D])
        xg = sb("xg", [P, 2, D])
        fix = sb("fix", [P, 2 * D])
        fix2 = sb("fix2", [P, D])
        yidx = sb("yidx", [P, 2], I32)
        flag_i = sb("flag_i", [1, 1], I32)
        flag_bc = sb("flag_bc", [P, 1])

        ps_agg = psum("ps_agg", [P, 2, 512])
        ps_x2 = psum("ps_x2", [P, 512])
        ps_tr = psum("ps_tr", [P, 512])
        ps_in = psum("ps_in", [P, 512])
        ps_h = psum("ps_h", [P, FC, P])
        ps_y = psum("ps_y", [P, 512])

        ident = cst[:, C_IDENT:C_IDENT + P]
        tri = cst[:, C_TRI:C_TRI + P]
        iota = cst[:, C_IOTA:C_IOTA + WIN]
        rank8 = cst[:, C_RANK:C_RANK + E8]

        def w1_at(b):
            return wsl[:, b, 0:KD * F].rearrange("p (k f) -> p k f", k=KD)

        def w2_at(b):
            return wsl[:, b, KD * F:KD * F + FC * D].rearrange("p (c d) -> p c d", c=FC)

        def b1_at(b):
            return wsl[:, b, KD * F + FC * D:KD * F + FC * D + FC]

        def b2_at(b):
            return wsl[:, b, WSZ - D:WSZ]

        ln_space = wsl[:, :, :].rearrange("p a b -> p (a b)")

        def ln_buf(u):
            return ln_space[:, u * LN_TILES * D:(u + 1) * LN_TILES * D].rearrange("p (t d) -> p t d", d=D)

        ln_small = sb("ln_small", [P, LN_BUFS, LN_TILES, 10])
        msg_flat = msg[:, :, :].rearrange("p g d -> p (g d)")
        dst_i = msg_flat[:, 0:COLS].bitcast(I32)
        lim_sb = msg_flat[:, COLS:COLS + 3 * (NG + 1)]
        chk = msg_flat[:, COLS + 3 * (NG + 1):COLS + 6 * (NG + 1) + 8]

        s_const = sem("s_const")
        s_edges = sem("s_edges")
        s_memset = sem("s_memset")
        s_lnx = [sem(f"s_lnx{u}") for u in range(LN_BUFS)]
        s_lnmv = sem("s_lnmv")
        s_lnsd = sem("s_lnsd")
        s_lnrs = sem("s_lnrs")
        s_lny = sem("s_lny")
        s_lnst = [sem(f"s_lnst{u}") for u in range(LN_BUFS)]
        s_lnc = sem("s_lnc")
        s_pre = sem("s_pre")
        s_prepe = sem("s_prepe")
        s_flag = sem("s_flag")
        g_idx, g_msg, g_onehot, g_mm, g_dve = (sem(q) for q in ("g_idx", "g_msg", "g_onehot", "g_mm", "g_dve"))
        s_idx = [sem(f"s_idx{q}") for q in range(3)]
        s_onehot = [sem(f"s_onehot{q}") for q in range(3)]
        s_msg = [sem(f"s_msg{q}") for q in range(3)]
        s_mm = [sem(f"s_mm{q}") for q in range(3)]
        s_added = [sem(f"s_added{q}") for q in range(3)]
        s_eq = sem("s_eq")
        s_aggS, s_n1, s_xt, s_x2, s_x2st = (sem(q) for q in ("s_aggS", "s_n1", "s_xt", "s_x2", "s_x2st"))
        s_nlink, s_mv, s_sd, s_h = (sem(q) for q in ("s_nlink", "s_mv", "s_sd", "s_h"))
        s_tr, s_hTs, s_log, s_ls, s_exp, s_choice, s_rank, s_route, s_scat = (
            sem(q) for q in ("s_tr", "s_hTs", "s_log", "s_ls", "s_exp", "s_choice", "s_rank", "s_route", "s_scat"))
        s_slink, s_plan, s_pad, s_dummy = (sem(q) for q in ("s_slink", "s_plan", "s_pad", "s_dummy"))
        s_hin = [sem(f"s_hin{b}") for b in range(2)]
        s_w = [sem(f"s_w{b}") for b in range(2)]
        s_yst = [sem(f"s_yst{b}") for b in range(2)]
        s_ft, s_hTf, s_l1, s_relu, s_l2, s_y = (sem(q) for q in ("s_ft", "s_hTf", "s_l1", "s_relu", "s_l2", "s_y"))
        s_yidx, s_flink, s_fin = (sem(q) for q in ("s_yidx", "s_flink", "s_fin"))
        s_yg = [sem(f"s_yg{b}") for b in range(2)]
        s_xg = [sem(f"s_xg{b}") for b in range(2)]
        s_out = [sem(f"s_out{b}") for b in range(2)]
        s_held = {q: sem("s_held_" + q) for q in ("sp", "act", "pe", "dve", "pool")}

        def known(value):
            return isinstance(value, int)

        def later(value):
            return not (known(value) and value == 0)

        def hold(eng, name, semaphore, value):
            eng.wait_ge(semaphore, value)
            if not known(value):
                eng.sem_inc(s_held[name], 1)

        class Links:

            def __init__(self, eng, name, semaphore, start):
                self.eng, self.name, self.semaphore, self.start, self.n = eng, name, semaphore, start, 0

            def mark(self, instruction):
                instruction.then_inc(self.semaphore, 1)
                self.n += 1

            def wait(self):
                hold(self.eng, self.name, self.semaphore, self.start + self.n)

            def __call__(self, instruction):
                self.mark(instruction)
                self.wait()

        @contextmanager
        def iterations(eng, count):
            if count == 1:
                yield 0
            else:
                with eng.Fori(0, count) as t:
                    yield t

        def walk(eng, steps, sched=None):
            for count, it in TIMELINE:
                if "sched" in it:
                    if sched:
                        sched(it["sched"])
                    continue
                with iterations(eng, count) as t:
                    a = it["agg"] + t if "agg" in it else None
                    n = it["node"] + t if "node" in it else None
                    k = it["ffn"] + t * 2 if "ffn" in it else None
                    fs = [it["fin"] + t * it["fins"] + j for j in range(it["fins"])] if "fin" in it else []
                    steps(a, n, k, [(f, (it["fin"] + j) % 2) for j, f in enumerate(fs)], it)

        def rows_of(n):
            return LAST_ROWS if known(n) and n == NT - 1 else P

        def fins_before(s):
            before = TIMELINE[:[it.get("sched") for _, it in TIMELINE].index(s)]
            return sum(count * it.get("fins", 0) for count, it in before)

        def half(k, b):
            return (k - b) // 2

        def ln_stores(u):
            total = 16 * len([b for b in range(LN_FULL) if b % LN_BUFS == u])
            left = N - LN_FULL * LN_ROWS
            if u == LN_FULL % LN_BUFS:
                total += 16 * ((left // P > 0) + (left % P > 0))
            return total

        def ln_rows(b, t):
            left = N - LN_FULL * LN_ROWS
            return left % P if known(b) and b == LN_FULL and t == left // P else P

        def ln_batches(eng, batch):
            rounds = LN_FULL // LN_BUFS
            if rounds:
                with iterations(eng, rounds) as r:
                    for u in range(LN_BUFS):
                        batch(r * LN_BUFS + u, u, LN_TILES, r * 16 + 16)
            for b in range(rounds * LN_BUFS, LN_FULL):
                batch(b, b % LN_BUFS, LN_TILES, 16 * (b // LN_BUFS + 1))
            left = N - LN_FULL * LN_ROWS
            if left:
                u = LN_FULL % LN_BUFS
                batch(LN_FULL, u, -(-left // P), ln_stores(u))

        LINKS_NODE, LINKS_FIN, LINKS_SCHED = 18, 6, 46
        block = ctx.enter_context(nc.Block())

        @block.sync
        def _(sp):
            for dst, source in ((cst[:, :], consts), (wg_sb[:, :, :], w_gnn), (bg_sb[:, :], b_gnn),
                                (gw_sb[:, :, :], gate_w), (gb_sb[:, :], gate_b.partition_broadcast(P))):
                sp.dma_start(dst, source).then_inc(s_const, 16)
            for dst, source in ((dst_i, dst_t), (lim_sb, limits), (src_sb[:, :], src_t), (wgt[:, :], w_t)):
                sp.dma_start(dst, source).then_inc(s_edges, 16)

            def load(b, u, again):
                if again is not None:
                    hold(sp, "sp", s_lnst[u], again)
                sp.dma_start(ln_buf(u), x[bass.ds(b * LN_ROWS, LN_ROWS), :].rearrange(
                    "(p t) d -> p t d", t=LN_TILES)).then_inc(s_lnx[u], 16)

            rounds = LN_FULL // LN_BUFS
            if rounds:
                for u in range(LN_BUFS):
                    load(u, u, None)
            if rounds > 1:
                with sp.Fori(1, rounds) as r:
                    for u in range(LN_BUFS):
                        load(r * LN_BUFS + u, u, r * 16)
            for b in range(rounds * LN_BUFS, LN_FULL):
                load(b, b % LN_BUFS, 16 * (b // LN_BUFS))
            b, u = LN_FULL, LN_FULL % LN_BUFS
            left = N - LN_FULL * LN_ROWS
            if b >= LN_BUFS:
                hold(sp, "sp", s_lnst[u], 16 * (b // LN_BUFS))
            if left // P:
                sp.dma_start(ln_buf(u)[:, 0:left // P, :], x[b * LN_ROWS:b * LN_ROWS + left // P * P, :].rearrange(
                    "(p t) d -> p t d", t=left // P)).then_inc(s_lnx[u], 16)
            if left % P:
                sp.dma_start(ln_buf(u)[0:left % P, left // P, :], x[N - left % P:N, :]).then_inc(s_lnx[u], 16)
            for s in range(S):
                row = BASE[s] + E8 * CAPS[s]
                sp.dma_start(hbuf[row:row + P, :], zeros).then_inc(s_dummy, 16)
            for u in range(LN_BUFS):
                hold(sp, "sp", s_lnst[u], ln_stores(u))

            def steps(a, n, k, fins, it):
                if k is not None:
                    for b in range(2):
                        kk = k + b
                        expert = sp.value_load(plan[0:1, bass.ds(kk * 4, 1)], min_val=0, max_val=E8 - 1)
                        first = sp.value_load(plan[0:1, bass.ds(kk * 4 + 1, 1)], min_val=0, max_val=ROWS - P)
                        changed = sp.value_load(plan[0:1, bass.ds(kk * 4 + 3, 1)], min_val=0, max_val=1)
                        expert, first = sp.snap(expert), sp.snap(first)
                        if not known(k):
                            hold(sp, "sp", s_ft, kk - 1)
                            hold(sp, "sp", s_y, kk - 1)
                        elif k:
                            sp.wait_ge(s_ft, kk - 1)
                            sp.wait_ge(s_y, kk - 1)
                        sp.dma_start(hin[:, b, :], hbuf[bass.ds(first, P), :]).then_inc(s_hin[b], 16)
                        with sp.If(changed >= 1):
                            sp.dma_start(w1_at(b), w1[bass.ds(expert, 1)].rearrange(
                                "e p k f -> p (e k) f")).then_inc(s_w[b], 16)
                            sp.dma_start(w2_at(b), w2[bass.ds(expert, 1)].rearrange(
                                "e p c d -> p (e c) d")).then_inc(s_w[b], 16)
                            sp.dma_start(b1_at(b), b1[bass.ds(expert, 1)].rearrange(
                                "e p c -> p (e c)")).then_inc(s_w[b], 16)
                            sp.dma_start(b2_at(b), b2[bass.ds(expert, 1)].rearrange(
                                "e p d -> p (e d)")).then_inc(s_w[b], 16)
                        with sp.Else():
                            sp.sem_inc(s_w[b], 64)
                if n is not None:
                    if later(n):
                        hold(sp, "sp", s_x2st, n * 16)
                        hold(sp, "sp", s_h, n)
                    r = rows_of(n)
                    sp.dma_start(xt[0:r, :], x[bass.ds(n * P, r), :]).then_inc(s_xt, 16)
                    hold(sp, "sp", s_x2, n + 1)
                    sp.dma_start(x2_dram[bass.ds(n * P, r), :], xt[0:r, :]).then_inc(s_x2st, 16)
                for f, b in fins:
                    r = rows_of(f)
                    if known(f) and f < 2:
                        hold(sp, "sp", s_x2st, 16 * min(SEG[0], NT))
                    else:
                        hold(sp, "sp", s_out[b], half(f, b) * 16)
                    sp.dma_start(xg[0:r, b, :], x2_dram[bass.ds(f * P, r), :]).then_inc(s_xg[b], 16)

            def sched(s):
                if s == S:
                    return
                hold(sp, "sp", s_plan, s + 1)
                hold(sp, "sp", s_x2st, 16 * sum(SEG[:s + 1]))
                for e in range(E8):
                    row = sp.value_load(pads[0:1, s * E8 + e:s * E8 + e + 1], min_val=0, max_val=ROWS - P)
                    sp.dma_start(hbuf[bass.ds(row, P), :], zeros).then_inc(s_pad, 16)
                sp.wait_ge(s_pad, 16 * E8 * (s + 1))
                sp.wait_ge(s_dummy, 16 * S)
                sp.wait_ge(s_scat, 16 * sum(SEG[:s + 1]))

            hold(sp, "sp", s_flag, 1)
            walk(sp, steps, sched)
            for q in range(2):
                sp.wait_ge(s_out[q], 16 * ((NT + 1 - q) // 2))

        @block.gpsimd
        def _(pool):
            for u in range(LN_BUFS):
                pool.wait_ge(s_lnst[u], ln_stores(u))
            pool.wait_ge(s_flag, 1)
            fast = pool.value_load(flag_i[0:1, 0:1], min_val=0, max_val=1)
            with pool.If(fast < 1):
                with pool.Fori(0, NG) as g:
                    hold(pool, "pool", g_idx, g + 1)
                    for j in range(G):
                        pool.indirect_dma_start(
                            out=msg[:, j, :], out_offset=None, in_=ln_dram,
                            in_offset=bass.IndirectOffsetOnAxis(ap=idx[:, j:j + 1], axis=0)).then_inc(g_msg, 16)
            with pool.Else():
                pool.sem_inc(s_held["pool"], 1)

            def steps(a, n, k, fins, it):
                if a is not None:
                    for q in range(3):
                        hold(pool, "pool", s_idx[q], a + 1)
                        for j in range(OFF[q], OFF[q] + SUBS[q]):
                            pool.indirect_dma_start(
                                out=msg[:, j, :], out_offset=None, in_=ln_dram,
                                in_offset=bass.IndirectOffsetOnAxis(ap=idx[:, j:j + 1], axis=0)
                            ).then_inc(s_msg[q], 16)
                if n is not None:
                    r = rows_of(n)
                    hold(pool, "pool", s_route, n + 1)
                    pool.indirect_dma_start(
                        out=hbuf, out_offset=bass.IndirectOffsetOnAxis(ap=slot_i[0:r, 0:1], axis=0),
                        in_=hrow[0:r, :], in_offset=None).then_inc(s_scat, 16)
                for f, b in fins:
                    r = rows_of(f)
                    hold(pool, "pool", s_yidx, f + 1)
                    if known(f):
                        outputs_of(1 if it["source"] == 0 else S if it["source"] == 2 else S - 1)
                    pool.indirect_dma_start(
                        out=yg[0:r, b, :], out_offset=None, in_=ybuf[it["source"]],
                        in_offset=bass.IndirectOffsetOnAxis(ap=yidx[0:r, b:b + 1], axis=0)).then_inc(s_yg[b], 16)

            def outputs_of(segments):
                for q in range(2):
                    pool.wait_ge(s_yst[q], 16 * (sum(FFN[:segments]) // 2))

            def sched(s):
                if s >= S - 1:
                    outputs_of(s)

            walk(pool, steps, sched)

        @block.scalar
        def _(act):
            act.wait_ge(s_memset, 2)

            def batch(b, u, tiles, arrived):
                small = ln_small[:, u, 0:tiles, :]
                hold(act, "act", s_lnmv, b + 1)
                nc.scalar.activation(small[:, :, 8], small[:, :, 7], ACT.Sqrt, bias=eps[:, 0:1]).then_inc(s_lnsd, 1)
                hold(act, "act", s_lnrs, b + 1)
                for t in range(tiles):
                    r = ln_rows(b, t)
                    last = nc.scalar.activation(ln_buf(u)[0:r, t, :], ln_buf(u)[0:r, t, :], ACT.Identity,
                                                bias=small[0:r, t, 9:10], scale=small[0:r, t, 8:9])
                last.then_inc(s_lny, 1)
                hold(act, "act", s_lny, b + 1)
                if known(b) and b == LN_FULL:
                    left = N - LN_FULL * LN_ROWS
                    if left // P:
                        act.dma_start(ln_dram[b * LN_ROWS:b * LN_ROWS + left // P * P, :].rearrange(
                            "(p t) d -> p t d", t=left // P), ln_buf(u)[:, 0:left // P, :]).then_inc(s_lnst[u], 16)
                    if left % P:
                        act.dma_start(ln_dram[N - left % P:N, :], ln_buf(u)[0:left % P, left // P, :]
                                      ).then_inc(s_lnst[u], 16)
                else:
                    act.dma_start(ln_dram[bass.ds(b * LN_ROWS, LN_ROWS), :].rearrange(
                        "(p t) d -> p t d", t=LN_TILES), ln_buf(u)).then_inc(s_lnst[u], 16)

            ln_batches(act, batch)

            def relu(k, b):
                hold(act, "act", s_w[b], half(k, b) * 64 + 64)
                for c in range(FC):
                    if c % HALF == 0:
                        hold(act, "act", s_l1, k * 2 + c // HALF + 1)
                    ins = nc.scalar.activation(hmid[:, c, :], ps_h[:, c, :], ACT.Relu, bias=b1_at(b)[:, c:c + 1])
                    if c % HALF == HALF - 1:
                        ins.then_inc(s_relu, 1)

            def steps(a, n, k, fins, it):
                if n is not None:
                    hold(act, "act", s_added[2], min(n + LAG, NG) if known(n) else n + LAG)
                    if later(n):
                        hold(act, "act", s_n1, n)
                    nc.scalar.copy(aggS[:, :, :], aggT[:, :, bass.ds(n * P, P)]).then_inc(s_aggS, 1)
                    hold(act, "act", s_mv, n + 1)
                    nc.scalar.activation(sd[:, :], mv[:, 1:2], ACT.Sqrt, bias=eps[:, 0:1]).then_inc(s_sd, 1)
                if k is not None:
                    relu(k, 0)
                if n is not None:
                    hold(act, "act", s_tr, n + 1)
                    if later(n):
                        hold(act, "act", s_log, n)
                    nc.scalar.copy(hTs[:, :, :], ps_tr[:, 0:D].rearrange("p (k t) -> p k t", k=KD)
                                   ).then_inc(s_hTs, 1)
                    hold(act, "act", s_ls, n + 1)
                    nc.scalar.activation(rt[:, 2 * E8:3 * E8], rt[:, E8:2 * E8], ACT.Exp,
                                         accum_out=sc[:, 1:2]).then_inc(s_exp, 1)
                if k is not None:
                    relu(k + 1, 1)
                    for b in range(2):
                        kk = k + b
                        hold(act, "act", s_y, kk + 1)
                        act.dma_start(ybuf[it["to"]][bass.ds((kk - KBUF[it["to"]]) * P, P), :], yrow[:, b, :]
                                      ).then_inc(s_yst[b], 16)
                for f, b in fins:
                    r = rows_of(f)
                    hold(act, "act", s_fin, f + 1)
                    act.dma_start(out[bass.ds(f * P, r), :], xg[0:r, b, :]).then_inc(s_out[b], 16)

            walk(act, steps)

        @block.tensor
        def _(pe):
            pe.wait_ge(s_const, 80)
            pe.wait_ge(s_memset, 2)
            pe.wait_ge(s_pre, 1)
            for q in range(3):
                firsts = rel[0:1, OFF[q]:OFF[q] + NG * G + 1:G]
                last = nc.tensor.matmul(ps_h[:, q, 0:NG + 1], ones[0:1, :], firsts, start=True, stop=True)
            last.then_inc(s_prepe, 1)
            pe.wait_ge(s_pre, 2)
            nc.tensor.transpose(ps_tr[0:1, 0:P], chk[:, 0:1], ident).then_inc(s_prepe, 1)
            pe.wait_ge(s_pre, 3)
            nc.tensor.matmul(ps_tr[:, P:P + 1], ones[0:1, :], chk[0:1, 2:3], start=True, stop=True
                             ).then_inc(s_prepe, 1)

            pe.wait_ge(s_flag, 1)
            fast = pe.value_load(flag_i[0:1, 0:1], min_val=0, max_val=1)
            with pe.If(fast < 1):
                with pe.Fori(0, NG) as g:
                    hold(pe, "pe", g_msg, g * (16 * G) + 16 * G)
                    with pe.Fori(0, WINDOWS) as w:
                        hold(pe, "pe", g_onehot, g * WINDOWS + w + 1)
                        for k in range(KD):
                            for j in range(G):
                                last = nc.tensor.matmul(ps_agg[:, 0, k * WIN:(k + 1) * WIN],
                                                        msg[:, j, k * P:(k + 1) * P], onehot[:, j, :],
                                                        start=j == 0, stop=j == G - 1)
                        last.then_inc(g_mm, 1)
            with pe.Else():
                pe.sem_inc(s_held["pe"], 1)

            def sub(a, q):
                hold(pe, "pe", s_msg[q], a * (16 * SUBS[q]) + 16 * SUBS[q])
                hold(pe, "pe", s_onehot[q], a + 1)
                if q == 2:
                    hold(pe, "pe", s_added[0], a + 1)
                elif later(a):
                    hold(pe, "pe", s_added[2 - q], a)
                for k in range(KD):
                    for j in range(OFF[q], OFF[q] + SUBS[q]):
                        last = nc.tensor.matmul(ps_agg[:, q % 2, k * WIN:(k + 1) * WIN],
                                                msg[:, j, k * P:(k + 1) * P], onehot[:, j, :],
                                                start=j == OFF[q], stop=j == OFF[q] + SUBS[q] - 1)
                last.then_inc(s_mm[q], 1)

            def gnn(n):
                hold(pe, "pe", s_aggS, n + 1)
                if later(n):
                    hold(pe, "pe", s_x2, n)
                for k in range(KD):
                    nc.tensor.matmul(ps_x2[:, 0:D], aggS[:, k, :], wg_sb[:, k, :], start=k == 0, stop=False)
                nc.tensor.matmul(ps_x2[:, 0:D], ones[0:1, :], bg_sb[0:1, :], start=False, stop=True
                                 ).then_inc(s_n1, 1)

            def turn_node(n):
                hold(pe, "pe", s_h, n + 1)
                if later(n):
                    hold(pe, "pe", s_route, n)
                for k in range(KD):
                    last = nc.tensor.transpose(ps_tr[:, k * P:(k + 1) * P], hrow[:, k * P:(k + 1) * P], ident)
                last.then_inc(s_tr, 1)

            def logits(n):
                hold(pe, "pe", s_hTs, n + 1)
                for k in range(KD):
                    last = nc.tensor.matmul(ps_tr[:, D:D + E8], hTs[:, k, :], gw_sb[:, k, :],
                                            start=k == 0, stop=k == KD - 1)
                last.then_inc(s_log, 1)

            def ranks(n):
                r = rows_of(n)
                hold(pe, "pe", s_choice, n + 1)
                choice = rt[0:r, 3 * E8:4 * E8]
                nc.tensor.matmul(ps_tr[:, D + E8:D + 2 * E8], tri[0:r, :], choice, start=True, stop=True)
                nc.tensor.matmul(ps_tr[:, D + 2 * E8:D + 3 * E8], ones[0:r, :], choice, start=True, stop=True
                                 ).then_inc(s_rank, 1)

            def turn_ffn(k, b):
                hold(pe, "pe", s_hin[b], half(k, b) * 16 + 16)
                if not (known(k) and k == 0):
                    hold(pe, "pe", s_hTf, k)
                for q in range(KD):
                    last = nc.tensor.transpose(ps_in[:, q * P:(q + 1) * P], hin[:, b, q * P:(q + 1) * P], ident)
                last.then_inc(s_ft, 1)

            def layer1(k, b):
                hold(pe, "pe", s_hTf, k + 1)
                hold(pe, "pe", s_w[b], half(k, b) * 64 + 64)
                for c in range(FC):
                    for q in range(KD):
                        last = nc.tensor.matmul(ps_h[:, c, :], w1_at(b)[:, q, c * P:(c + 1) * P], hTf[:, q, :],
                                                start=q == 0, stop=q == KD - 1)
                    if c % HALF == HALF - 1:
                        last.then_inc(s_l1, 1)

            def layer2(k, b):
                if later(k):
                    hold(pe, "pe", s_y, k)
                for c in range(FC):
                    if c % HALF == 0:
                        hold(pe, "pe", s_relu, k * 2 + c // HALF + 1)
                    last = nc.tensor.matmul(ps_y[:, 0:D], hmid[:, c, :], w2_at(b)[:, c, :],
                                            start=c == 0, stop=c == FC - 1)
                last.then_inc(s_l2, 1)

            def steps(a, n, k, fins, it):
                if n is not None:
                    gnn(n)
                if k is not None:
                    turn_ffn(k, 0)
                    layer1(k, 0)
                if a is not None:
                    sub(a, 0)
                if k is not None:
                    layer2(k, 0)
                if n is not None:
                    turn_node(n)
                if k is not None:
                    turn_ffn(k + 1, 1)
                if a is not None:
                    sub(a, 1)
                if n is not None:
                    logits(n)
                if k is not None:
                    layer1(k + 1, 1)
                if n is not None:
                    ranks(n)
                if a is not None:
                    sub(a, 2)
                if k is not None:
                    layer2(k + 1, 1)

            walk(pe, steps)

        @block.vector
        def _(dve):
            dve.memset(ones[:, :], 1.0).then_inc(s_memset, 1)
            dve.memset(eps[:, :], EPS).then_inc(s_memset, 1)
            dve.wait_ge(s_memset, 2)

            LINKS_LN = 3

            def batch(b, u, tiles, arrived):
                link = Links(dve, "dve", s_lnc, b * LINKS_LN)
                small = ln_small[:, u, 0:tiles, :]
                hold(dve, "dve", s_lnx[u], arrived)
                for t in range(tiles):
                    r = ln_rows(b, t)
                    last = dve.bn_stats(small[0:r, t, 0:6], ln_buf(u)[0:r, t, :])
                link(last)
                for t in range(tiles):
                    r = ln_rows(b, t)
                    last = dve.bn_aggr(small[0:r, t, 6:8], small[0:r, t, 0:6])
                last.then_inc(s_lnmv, 1)
                hold(dve, "dve", s_lnsd, b + 1)
                link(dve.reciprocal(small[:, :, 8], small[:, :, 8]))
                link(dve.scalar_tensor_tensor(out=small[:, :, 9], in0=small[:, :, 6], scalar=-1.0,
                                              in1=small[:, :, 8], op0=ALU.mult, op1=ALU.mult))
                dve.sem_inc(s_lnrs, 1)

            dve.memset(ln_small[:, :, :, :], 0.0).then_inc(s_memset, 1)
            dve.wait_ge(s_memset, 3)

            link = Links(dve, "dve", sem("s_prelink"), 0)
            dve.wait_ge(s_const, 80)
            dve.wait_ge(s_edges, 64)
            link(dve.tensor_copy(rel[:, :], dst_i))
            dve.sem_inc(s_pre, 1)
            dve.wait_ge(s_prepe, 1)
            firsts = base_bc[:, :].rearrange("p (g q) -> p g q", q=3)
            for q in range(3):
                link.mark(dve.tensor_copy(firsts[:, :, q], ps_h[:, q, 0:NG + 1]))
            link.wait()
            link.mark(dve.tensor_copy(base_i[0:1, :], base_bc[0:1, :]))
            rel3 = rel[:, :].rearrange("p (g j) -> p g j", j=G)
            for q in range(3):
                part = rel3[:, :, OFF[q]:OFF[q] + SUBS[q]]
                link.mark(dve.tensor_tensor(part, part, firsts[:, :, q:q + 1].to_broadcast([P, NG + 1, SUBS[q]]),
                                            ALU.subtract))
            link(dve.tensor_tensor(chk[:, 8:8 + 3 * (NG + 1)], base_bc[:, :], lim_sb, ALU.subtract))
            link.mark(dve.tensor_reduce(chk[:, 3:4], rel[:, :], AX_X, ALU.min))
            link.mark(dve.tensor_reduce(chk[:, 4:5], rel[:, :], AX_X, ALU.max))
            link(dve.tensor_reduce(chk[:, 5:6], chk[:, 8:8 + 3 * (NG + 1)], AX_X, ALU.min))
            link(dve.tensor_scalar(chk[:, 4:5], chk[:, 4:5], -1.0, float(WIN - 1), ALU.mult, ALU.add))
            link(dve.tensor_tensor(chk[:, 3:4], chk[:, 3:4], chk[:, 4:5], ALU.min))
            link(dve.tensor_tensor(chk[:, 0:1], chk[:, 3:4], chk[:, 5:6], ALU.min))
            dve.sem_inc(s_pre, 1)
            dve.wait_ge(s_prepe, 2)
            link(dve.tensor_reduce(chk[0:1, 1:2], ps_tr[0:1, 0:P], AX_X, ALU.min))
            link(dve.tensor_scalar(chk[0:1, 2:3], chk[0:1, 1:2], 0.0, None, ALU.is_ge))
            dve.sem_inc(s_pre, 1)
            link.mark(dve.tensor_copy(flag_i[0:1, 0:1], chk[0:1, 2:3]))
            dve.wait_ge(s_prepe, 3)
            link.mark(dve.tensor_copy(flag_bc[:, :], ps_tr[:, P:P + 1]))
            link.mark(dve.memset(seen[:, :], 0.0))
            link.mark(dve.memset(hrow[:, :], 0.0))
            link.mark(dve.memset(xt[:, :], 0.0))
            link.mark(dve.tensor_copy(offs[:, :], cst[:, C_SEG:C_SEG + E8]))
            link(dve.memset(aggT[:, :, :], 0.0))

            ln_batches(dve, batch)
            dve.sem_inc(s_flag, 1)

            fast = dve.value_load(flag_i[0:1, 0:1], min_val=0, max_val=1)
            with dve.If(fast < 1):
                at = fix[:, 0:G]
                with dve.Fori(0, NG) as g:
                    glink = Links(dve, "dve", g_dve, g * (5 + 4 * WINDOWS))
                    glink(dve.tensor_copy(idx[:, :], src_sb[:, bass.ds(g * G, G)]))
                    dve.sem_inc(g_idx, 1)
                    for q in range(3):
                        glink.mark(dve.tensor_tensor(
                            at[:, OFF[q]:OFF[q] + SUBS[q]], rel[:, bass.ds(g * G + OFF[q], SUBS[q])],
                            base_bc[:, bass.ds(g * 3 + q, 1)].to_broadcast([P, SUBS[q]]), ALU.add))
                    glink(dve.tensor_copy(fix[:, 32:32 + G], wgt[:, bass.ds(g * G, G)]))
                    with dve.Fori(0, WINDOWS) as w:
                        wlink = Links(dve, "dve", g_dve, g * (5 + 4 * WINDOWS) + w * 4 + 5)
                        wlink(dve.tensor_tensor(
                            onehot[:, :, :], iota.unsqueeze(1).to_broadcast([P, G, WIN]),
                            at.unsqueeze(2).to_broadcast([P, G, WIN]), ALU.is_equal))
                        wlink(dve.tensor_tensor(
                            onehot[:, :, :], onehot[:, :, :],
                            fix[:, 32:32 + G].unsqueeze(2).to_broadcast([P, G, WIN]), ALU.mult))
                        dve.sem_inc(g_onehot, 1)
                        hold(dve, "dve", g_mm, g * WINDOWS + w + 1)
                        columns = aggT[:, :, bass.ds(w * WIN, WIN)]
                        wlink(dve.tensor_tensor(
                            columns, columns, ps_agg[:, 0, 0:KD * WIN].rearrange("p (k c) -> p k c", k=KD), ALU.add))
                        wlink(dve.tensor_scalar(at, at, -float(WIN), None, ALU.add))
            with dve.Else():
                dve.sem_inc(s_held["dve"], 1)
            dve.tensor_scalar(wgt[:, :], wgt[:, :], flag_bc[:, 0:1], None, ALU.mult).then_inc(s_flag, 1)
            dve.wait_ge(s_flag, 2)

            def prep(a, q):
                n = SUBS[q]
                col = a * G + OFF[q]
                dve.tensor_copy(idx[:, OFF[q]:OFF[q] + n], src_sb[:, bass.ds(col, n)]).then_inc(s_idx[q], 1)
                hot = onehot[:, OFF[q]:OFF[q] + n, :]
                dve.tensor_tensor(hot, iota.unsqueeze(1).to_broadcast([P, n, WIN]),
                                  rel[:, bass.ds(col, n)].unsqueeze(2).to_broadcast([P, n, WIN]), ALU.is_equal
                                  ).then_inc(s_eq, 1)
                hold(dve, "dve", s_eq, a * 3 + q + 1)
                dve.tensor_tensor(hot, hot, wgt[:, bass.ds(col, n)].unsqueeze(2).to_broadcast([P, n, WIN]),
                                  ALU.mult).then_inc(s_onehot[q], 1)

            def sub(a, q):
                first = dve.snap(dve.value_load(base_i[0:1, bass.ds(a * 3 + q, 1)], min_val=0, max_val=N - 1))
                hold(dve, "dve", s_mm[q], a + 1)
                prev, val = (2, a) if q == 0 else (q - 1, a + 1)
                if not (known(a) and a == 0 and q == 0):
                    hold(dve, "dve", s_added[prev], val)
                columns = aggT[:, :, bass.ds(first, WIN)]
                dve.tensor_tensor(columns, columns, ps_agg[:, q % 2, 0:KD * WIN].rearrange("p (k c) -> p k c", k=KD), ALU.add
                                  ).then_inc(s_added[q], 1)
                if known(a):
                    prep(a + 1, q)
                else:
                    prep(a + 1, q)

            def norm_a(n, link):
                hold(dve, "dve", s_n1, n + 1)
                hold(dve, "dve", s_xt, n * 16 + 16)
                link.mark(dve.tensor_tensor(xt[:, :], xt[:, :], ps_x2[:, 0:D], ALU.add))
                link.wait()
                dve.sem_inc(s_x2, 1)
                link(dve.bn_stats(st6[:, :], xt[:, :]))
                link(dve.bn_aggr(mv[:, :], st6[:, :]))
                dve.sem_inc(s_mv, 1)

            def norm_b(n, link):
                hold(dve, "dve", s_sd, n + 1)
                link(dve.reciprocal(rs[:, :], sd[:, :]))
                if later(n):
                    hold(dve, "dve", s_scat, n * 16)
                dve.tensor_scalar(hrow[:, :], xt[:, :], mv[:, 0:1], rs[:, 0:1], ALU.subtract, ALU.mult
                                  ).then_inc(s_h, 1)

            def cols8(j):
                return rt[:, j * E8:(j + 1) * E8]

            def route_a(n, link):
                hold(dve, "dve", s_log, n + 1)
                link(dve.tensor_tensor(cols8(0), ps_tr[:, D:D + E8], gb_sb[:, :], ALU.add))
                link(dve.tensor_reduce(sc[:, 0:1], cols8(0), AX_X, ALU.max))
                link.mark(dve.tensor_scalar(cols8(1), cols8(0), sc[:, 0:1], None, ALU.subtract))
                link(dve.scalar_tensor_tensor(out=cols8(4), in0=cols8(0), scalar=sc[:, 0:1], in1=rank8,
                                              op0=ALU.is_ge, op1=ALU.mult))
                dve.sem_inc(s_ls, 1)
                link(dve.tensor_reduce(sc[:, 2:3], cols8(4), AX_X, ALU.max))
                link(dve.tensor_scalar(cols8(3), rank8, sc[:, 2:3], None, ALU.is_equal))
                dve.sem_inc(s_choice, 1)

            def route_b(n, link):
                hold(dve, "dve", s_rank, n + 1)
                hold(dve, "dve", s_exp, n + 1)
                link(dve.tensor_tensor(cols8(5), ps_tr[:, D + E8:D + 2 * E8], seen[:, :], ALU.add))
                link.mark(dve.tensor_tensor(seen[:, :], seen[:, :], ps_tr[:, D + 2 * E8:D + 3 * E8], ALU.add))
                link.mark(dve.tensor_tensor(cols8(6), cols8(5), cols8(3), ALU.mult))
                link.mark(dve.reciprocal(sc[:, 3:4], sc[:, 1:2]))
                link(dve.tensor_tensor(cols8(5), cols8(5), offs[:, :], ALU.add))
                link.mark(dve.tensor_reduce(sc[:, 4:5], cols8(6), AX_X, ALU.add))
                link(dve.tensor_tensor(cols8(7), cols8(5), cols8(3), ALU.mult))
                link(dve.tensor_reduce(sc[:, 5:6], cols8(7), AX_X, ALU.add))
                dve.scalar_tensor_tensor(out=gain[:, bass.ds(n, 1)], in0=sc[:, 4:5], scalar=float(CAP),
                                         in1=sc[:, 3:4], op0=ALU.is_lt, op1=ALU.mult)
                dve.tensor_copy(slots[:, bass.ds(n, 1)], sc[:, 5:6])
                dve.tensor_copy(chosen[:, bass.ds(n, 1)], sc[:, 2:3])
                dve.tensor_copy(slot_i[:, :], sc[:, 5:6]).then_inc(s_route, 1)

            def copy_in(k):
                hold(dve, "dve", s_ft, k + 1)
                if not (known(k) and k == 0):
                    hold(dve, "dve", s_l1, k * 2)
                dve.tensor_copy(hTf[:, :, :], ps_in[:, 0:D].rearrange("p (k t) -> p k t", k=KD)).then_inc(s_hTf, 1)

            def expert_out(k, b):
                hold(dve, "dve", s_l2, k + 1)
                if not (known(k) and k < 2):
                    hold(dve, "dve", s_yst[b], half(k, b) * 16)
                dve.tensor_tensor(yrow[:, b, :], ps_y[:, 0:D], b2_at(b), ALU.add).then_inc(s_y, 1)

            def final_index(f, b):
                if not (known(f) and f < 2):
                    hold(dve, "dve", s_yg[b], half(f, b) * 16)
                else:
                    dve.wait_ge(s_route, SEG[0])
                dve.tensor_copy(yidx[:, b:b + 1], slots[:, bass.ds(f, 1)]).then_inc(s_yidx, 1)

            def final(f, b):
                r = rows_of(f)
                link = Links(dve, "dve", s_flink, f * LINKS_FIN)
                hold(dve, "dve", s_yg[b], half(f, b) * 16 + 16)
                hold(dve, "dve", s_xg[b], half(f, b) * 16 + 16)
                y, kept, low, high = yg[0:r, b, :], fix[0:r, 0:D], fix[0:r, D:2 * D], fix2[0:r, :]
                assert LINKS_FIN == 6
                link(dve.tensor_scalar(y, y, gain[0:r, bass.ds(f, 1)], None, ALU.mult))
                link.mark(dve.tensor_scalar(low, y, -FLT_MAX, -1e4, ALU.is_lt, ALU.mult))
                link.mark(dve.tensor_scalar(kept.bitcast(I32), y, 0.0, 0.0, ALU.mult, ALU.is_equal))
                link(dve.tensor_scalar(high, y, FLT_MAX, 1e4, ALU.is_gt, ALU.mult))
                link(dve.tensor_tensor(low, low, high, ALU.add))
                link(dve.copy_predicated(low, kept.bitcast(I32), y))
                dve.tensor_tensor(xg[0:r, b, :], xg[0:r, b, :], low, ALU.add).then_inc(s_fin, 1)

            def steps(a, n, k, fins, it):
                link = Links(dve, "dve", s_nlink, n * LINKS_NODE) if n is not None else None
                for f, b in fins[:2]:
                    final_index(f, b)
                if n is not None:
                    norm_a(n, link)
                if k is not None:
                    copy_in(k)
                if n is not None:
                    norm_b(n, link)
                if a is not None:
                    sub(a, 0)
                if k is not None:
                    expert_out(k, 0)
                    copy_in(k + 1)
                if a is not None:
                    sub(a, 1)
                if n is not None:
                    route_a(n, link)
                    route_b(n, link)
                    assert link.n == LINKS_NODE, link.n
                if a is not None:
                    sub(a, 2)
                if k is not None:
                    expert_out(k + 1, 1)
                for j, (f, b) in enumerate(fins):
                    final(f, b)
                    if j + 2 < len(fins):
                        final_index(*fins[j + 2])

            def sched(s):
                if s == S:
                    return
                T, K, k0 = SEG[s], FFN[s], sum(FFN[:s])
                link = Links(dve, "dve", s_slink, s * LINKS_SCHED)
                io = iota[:, :]
                rows, n8, nt, cum, shift = (fix2[:, j * 8:(j + 1) * 8] for j in range(5))
                ek, stk = (fix2[:, 64 + j * 64:64 + j * 64 + K] for j in range(2))
                segrow = cst[:, C_SEG + s * E8:C_SEG + (s + 1) * E8]
                dve.wait_ge(s_route, sum(SEG[:s + 1]))
                if fins_before(s):
                    dve.wait_ge(s_fin, fins_before(s))
                link(dve.tensor_tensor(rows, seen[:, :], offs[:, :], ALU.add))
                link.mark(dve.tensor_copy(pads[0:1, s * E8:(s + 1) * E8], rows[0:1, :]))
                link(dve.tensor_tensor(n8, rows, segrow, ALU.subtract))
                link(dve.tensor_scalar(n8, n8, 1.0 / P, None, ALU.mult))
                cmp = fix[:, 0:E8 * (T + 1)].rearrange("p (e q) -> p e q", e=E8)
                link(dve.tensor_tensor(cmp, io[:, 0:T + 1].unsqueeze(1).to_broadcast([P, E8, T + 1]),
                                       n8.unsqueeze(2).to_broadcast([P, E8, T + 1]), ALU.is_lt))
                link(dve.tensor_reduce(nt, cmp, AX_X, ALU.add))
                link(dve.tensor_copy(cum, nt))
                for e in range(1, E8):
                    link(dve.tensor_tensor(cum[:, e:e + 1], cum[:, e:e + 1], cum[:, e - 1:e], ALU.add))
                past = fix[:, 0:K * E8].rearrange("p (k e) -> p k e", e=E8)
                link(dve.tensor_tensor(past, cum.unsqueeze(1).to_broadcast([P, K, E8]),
                                       io[:, 0:K].unsqueeze(2).to_broadcast([P, K, E8]), ALU.is_le))
                link(dve.tensor_reduce(ek, past, AX_X, ALU.add))
                link(dve.tensor_tensor(past, past, nt.unsqueeze(1).to_broadcast([P, K, E8]), ALU.mult))
                link(dve.tensor_reduce(stk, past, AX_X, ALU.add))
                link(dve.tensor_tensor(stk, io[:, 0:K], stk, ALU.subtract))
                link(dve.tensor_scalar(stk, stk, float(P), float(BASE[s]), ALU.mult, ALU.add))
                link(dve.scalar_tensor_tensor(out=stk, in0=ek, scalar=float(CAPS[s]), in1=stk,
                                              op0=ALU.mult, op1=ALU.add))
                rows4 = plan[0:1, 4 * k0:4 * (k0 + K)].rearrange("p (k c) -> p k c", c=4)
                link.mark(dve.tensor_scalar(rows4[:, :, 1], stk[0:1, :], float(BASE[s] + E8 * CAPS[s]), None, ALU.min))
                link(dve.tensor_scalar(ek, ek, float(E8 - 1), None, ALU.min))
                link.mark(dve.tensor_copy(rows4[:, :, 0], ek[0:1, :]))
                link.mark(dve.memset(rows4[:, 0:2, 3], 1))
                link(dve.tensor_tensor(rows4[:, 2:K, 3], ek[0:1, 2:K], ek[0:1, 0:K - 2], ALU.not_equal))
                dve.sem_inc(s_plan, 1)
                link(dve.tensor_tensor(shift, cum, nt, ALU.subtract))
                link(dve.tensor_scalar(shift, shift, float(P), float(P * (k0 - KBUF[buffer_of(s, S - 1)])),
                                       ALU.mult, ALU.add))
                link(dve.tensor_tensor(shift, shift, segrow, ALU.subtract))
                n0 = sum(SEG[:s])
                part, its = slots[:, n0:n0 + T], fix[:, 0:T]
                for e in range(E8):
                    link(dve.tensor_scalar(its, chosen[:, n0:n0 + T], float(E8 - e), shift[:, e:e + 1],
                                           ALU.is_equal, ALU.mult))
                    link(dve.tensor_tensor(part, part, its, ALU.add))
                assert link.n == LINKS_SCHED - 1, link.n
                if s + 1 < S:
                    link(dve.tensor_tensor(offs[:, :], cst[:, C_SEG + (s + 1) * E8:C_SEG + (s + 2) * E8],
                                           seen[:, :], ALU.subtract))

            for q in range(3):
                prep(0, q)
            walk(dve, steps, sched)


def kernel(**inputs):
    import numpy as np
    import concourse.bacc as bacc
    from concourse.bass_utils import run_bass_kernel_spmd

    x = np.ascontiguousarray(inputs["x"])
    N, D = x.shape
    edges = inputs["src"].shape[0]
    experts = inputs["L0_ffn_gate_w"].shape[1]
    F = inputs["L0_ffn_b1"].shape[1]
    z = layout_of(N, edges, experts)
    NT, COLS, S = z["tiles"], z["columns"], len(z["seg"])

    def by_tile(a, fill):
        a = np.asarray(a)
        whole = np.full(COLS * P, fill, a.dtype)
        whole[:edges] = a
        return np.ascontiguousarray(whole.reshape(COLS, P).T)

    consts = np.zeros((P, C_SEG + experts * S), np.float32)
    consts[:, C_IDENT:C_IDENT + P] = np.eye(P)
    consts[:, C_TRI:C_TRI + P] = np.triu(np.ones((P, P)), 1)
    consts[:, C_IOTA:C_IOTA + WIN] = np.arange(WIN)
    consts[:, C_RANK:C_RANK + experts] = experts - np.arange(experts)
    for s in range(S):
        consts[:, C_SEG + s * experts:C_SEG + (s + 1) * experts] = z["base"][s] + z["caps"][s] * np.arange(experts)
    limits = np.broadcast_to(np.repeat(P * (np.arange(NT + 1) - 1), 3).astype(np.float32), (P, 3 * (NT + 1)))

    def rows(a, chunk):
        a = np.asarray(a)
        *lead, r, c = a.shape
        return np.ascontiguousarray(np.moveaxis(a.reshape(*lead, r // P, P, c), -3, -2))

    arrays = dict(
        x=x, src_t=by_tile(inputs["src"], 0), dst_t=by_tile(inputs["dst"], N - 1),
        w_t=by_tile(inputs["edge_weight"], 0),
        w_gnn=rows(np.asarray(inputs["L0_gnn_W"]).T, P), b_gnn=np.asarray(inputs["L0_gnn_b"]).reshape(1, D),
        gate_w=rows(inputs["L0_ffn_gate_w"], P), gate_b=np.asarray(inputs["L0_ffn_gate_b"]),
        w1=rows(inputs["L0_ffn_w1"], P),
        b1=np.ascontiguousarray(np.asarray(inputs["L0_ffn_b1"]).reshape(experts, F // P, P).transpose(0, 2, 1)),
        w2=rows(inputs["L0_ffn_w2"], P),
        b2=np.ascontiguousarray(np.broadcast_to(np.asarray(inputs["L0_ffn_b2"])[:, None, :], (experts, P, D))),
        consts=consts, limits=np.ascontiguousarray(limits), zeros=np.zeros((P, D), np.float32),
    )
    nc = bacc.Bacc("TRN2", target_bir_lowering=False, num_devices=1)
    args = {name: nc.dram_tensor(f"in_{name}", a.shape, mybir.dt.from_np(a.dtype), kind="ExternalInput").ap()
            for name, a in arrays.items()}
    out = nc.dram_tensor("out_x", (N, D), F32, kind="ExternalOutput").ap()
    gnn_moe_kernel(nc, *args.values(), out, z)
    r = run_bass_kernel_spmd(nc, [{f"in_{name}": a for name, a in arrays.items()}], core_ids=[0])
    return r.results[0]["out_x"]
```

```python
from contextlib import ExitStack, contextmanager

import concourse.bass as bass
from concourse import mybir

P = 128
ALU = mybir.AluOpType
ACT = mybir.ActivationFunctionType
F32 = mybir.dt.float32
I32 = mybir.dt.int32
AX_X = mybir.AxisListType.X

WIN = 64
LAG = 2
CAPACITY_FACTOR = 1.25
EPS = 1e-5
FLT_MAX = 3.4028234663852886e38
LN_TILES = 7
LN_BUFS = 4
LN_ON_ACT = 5
LATE_FINS = 4
C_IDENT, C_TRI, C_IOTA, C_RANK, C_SEG = 0, 128, 256, 320, 328


def segments_of(tiles):
    if tiles >= 90:
        last = [25, 23, 22]
        return [tiles - sum(last)] + last
    return [tiles - tiles // 2, tiles // 2]


def capacity_of(tokens, experts):
    return max(1, -int(-CAPACITY_FACTOR * tokens // experts))


def layout_of(n, e, experts):
    tiles = -(-n // P)
    edge_tiles = -(-e // P)
    group = -(-edge_tiles // tiles)
    third = -(-group // 3)
    subs = [third, third, group - 2 * third]
    seg = segments_of(tiles)
    caps = [P * (t + 1) for t in seg]
    base = [0]
    for c in caps:
        base.append(base[-1] + (experts + 1) * c)
    return dict(tiles=tiles, group=group, subs=subs, seg=seg, caps=caps, base=base,
                columns=(tiles + 1) * group, ffn=[t + experts - 1 for t in seg])


def buffer_of(s, last):
    return 2 if s == last else min(s, 1)


def steps_of(tiles, seg, ffn):
    steps = [dict(agg=0), dict(agg=1)]
    node = k = f = todo = 0
    last = len(seg) - 1
    ends = [seg[0], sum(seg[:last]), tiles]

    def ffns(it, most, s):
        nonlocal k, todo
        n = min(most, todo)
        if n:
            it.update(ffn=k, ffns=n, to=buffer_of(s, last))
            k += n
            todo -= n

    def fins(it, most, ready, place):
        nonlocal f
        if f < ready:
            which = next(g for g in range(3) if f < ends[g])
            n = min(most, ends[which] - f)
            it.update(fin=f, fins=n, source=which, place=place)
            f += n

    for s, t in enumerate(seg):
        pace = [2, 1] if 2 * todo <= 3 * (t - 1) else [2]
        for j in range(t):
            it = dict(node=node)
            if node + LAG < tiles:
                it["agg"] = node + LAG
            if j:
                ffns(it, pace[(j - 1) % len(pace)], s - 1)
            if s == last and s > 1 and j:
                fins(it, 1, ends[0], 0)
            steps.append(it)
            node += 1
        while todo:
            steps.append({})
            ffns(steps[-1], 2, s - 1)
        steps.append(dict(sched=s))
        todo = ffn[s]
    while todo:
        it = {}
        ffns(it, 2, last)
        fins(it, LATE_FINS, ends[1], 1)
        steps.append(it)
    while f < ends[1]:
        steps.append({})
        fins(steps[-1], LATE_FINS, ends[1], 1)
    steps.append(dict(sched=len(seg)))
    while f < tiles:
        steps.append({})
        fins(steps[-1], LATE_FINS, tiles, 1)
    return steps


MOVING = ("agg", "node", "ffn", "fin")


def timeline_of(steps, tiles):
    def alone(i):
        it = steps[i]
        seen = [s for s in steps[:i]]
        new_place = "fin" in it and not any(
            "fin" in s and s["place"] == it["place"] and s["fins"] >= it["fins"] for s in seen)
        return ("sched" in it or it.get("agg") in (0, tiles - 1) or it.get("node") in (0, tiles - 1)
                or ("ffn" in it and it["ffn"] < 2) or new_place
                or ("fin" in it and it["fin"] + it["fins"] == tiles))

    def same(a, b, strides):
        return a.keys() == b.keys() and all(
            b[x] - a[x] == strides.setdefault(x, b[x] - a[x]) if x in MOVING else a[x] == b[x] for x in a)

    out, i = [], 0
    while i < len(steps):
        best = (1, 1, {})
        for period in (1, 2, 4):
            if i + 2 * period > len(steps) or any(alone(i + j) for j in range(period)):
                continue
            strides, count = {}, 1
            while i + (count + 1) * period <= len(steps) and not any(
                    alone(i + count * period + j) for j in range(period)) and all(
                    same(steps[i + (count - 1) * period + j], steps[i + count * period + j], strides)
                    for j in range(period)):
                count += 1
            if count > 1 and strides.get("ffn", 2) % 2 == 0 and count * period > best[0] * best[1]:
                best = (count, period, strides)
        count, period, strides = best
        out.append((count, steps[i:i + period], strides))
        i += count * period
    return out


def gnn_moe_kernel(nc, x, src_t, dst_t, w_t, w_gnn, b_gnn, gate_w, gate_b, w1, b1, w2, b2, consts, limits,
                   zeros, out, sizes):
    N, D = x.shape
    E8 = gate_w.shape[2]
    F = b1.shape[1] * b1.shape[2]
    FC = F // P
    KD = D // P
    HALF = FC // 2
    NT, G, SUBS, SEG, CAPS, BASE, COLS, FFN = (sizes[q] for q in (
        "tiles", "group", "subs", "seg", "caps", "base", "columns", "ffn"))
    OFF = [0, SUBS[0], SUBS[0] + SUBS[1]]
    NG = NT
    LAST_ROWS = N - (NT - 1) * P
    CAP = capacity_of(N, E8)
    NC = -(-(N + WIN) // WIN) * WIN
    WINDOWS = NC // WIN
    S = len(SEG)
    KTOT = sum(FFN)
    ROWS = BASE[-1]
    STEPS = steps_of(NT, SEG, FFN)
    TIMELINE = timeline_of(STEPS, NT)
    LN_ROWS = P * LN_TILES
    LN_FULL = N // LN_ROWS
    assert D == 2 * P and E8 == 8 and min(SEG) >= 7 and max(FFN) <= WIN and LAST_ROWS > 0 and G >= 2 * LATE_FINS + 3

    ln_dram = nc.dram_tensor("normed", (N, D), F32).ap()
    x2_dram = nc.dram_tensor("x_after_gnn", (N, D), F32).ap()
    hbuf = nc.dram_tensor("rows_by_expert", (ROWS, D), F32).ap()
    KBUF = [0, FFN[0], sum(FFN[:-1]), KTOT]
    ybuf = [nc.dram_tensor(f"expert_outputs{g}", (max(KBUF[g + 1] - KBUF[g], 1) * P, D), F32).ap() for g in range(3)]

    with ExitStack() as ctx:
        def sb(name, shape, dt=F32):
            return ctx.enter_context(nc.sbuf_tensor(name, shape, dt))

        def psum(name, shape):
            return ctx.enter_context(nc.psum_tensor(name, shape, F32))

        def sem(name):
            return ctx.enter_context(nc.semaphore(name))

        aggT = sb("aggT", [P, KD, NC])
        src_sb = sb("src_sb", [P, COLS], I32)
        rel = sb("rel", [P, COLS])
        wgt = sb("wgt", [P, COLS])
        base_bc = sb("base_bc", [P, 3 * (NG + 1)])
        base_i = sb("base_i", [1, 3 * (NG + 1)], I32)
        msg = sb("msg", [P, G, D])
        onehot = sb("onehot", [P, G, WIN])
        idx = sb("idx", [P, G], I32)
        cst = sb("cst", [P, C_SEG + E8 * S])
        ones = sb("ones", [P, P])
        eps = sb("eps", [P, 1])
        wg_sb = sb("wg_sb", [P, KD, D])
        bg_sb = sb("bg_sb", [P, D])
        gw_sb = sb("gw_sb", [P, KD, E8])
        gb_sb = sb("gb_sb", [P, E8])
        aggS = sb("aggS", [P, KD, P])
        xt = sb("xt", [P, D])
        hrow = sb("hrow", [P, D])
        hTs = sb("hTs", [P, KD, P])
        st6 = sb("st6", [P, 6])
        mv = sb("mv", [P, 2])
        sd = sb("sd", [P, 1])
        rs = sb("rs", [P, 1])
        rt = sb("rt", [P, 8 * E8])
        sc = sb("sc", [P, 8])
        slot_i = sb("slot_i", [P, 1], I32)
        slots = sb("slots", [P, NT])
        chosen = sb("chosen", [P, NT])
        gain = sb("gain", [P, NT])
        seen = sb("seen", [P, E8])
        offs = sb("offs", [P, E8])
        WSZ = KD * F + FC * D + FC + D
        wsl = sb("wsl", [P, 2, WSZ])
        hin = sb("hin", [P, 2, D])
        hTf = sb("hTf", [P, KD, P])
        hmid = sb("hmid", [P, FC, P])
        yrow = sb("yrow", [P, 2, D])
        plan = sb("plan", [1, 4 * KTOT], I32)
        pads = sb("pads", [1, E8 * S], I32)
        yg = sb("yg", [P, D])
        xg = sb("xg", [P, D])
        junk = sb("junk", [P, D])
        fix = sb("fix", [P, 2 * D])
        fix2 = sb("fix2", [P, D])
        yidx = sb("yidx", [P, 1 + LATE_FINS], I32)
        finite = sb("finite", [P, NT])
        flag_i = sb("flag_i", [1, 2], I32)
        flag_bc = sb("flag_bc", [P, 1])

        ps_agg = psum("ps_agg", [P, 2, 512])
        ps_x2 = psum("ps_x2", [P, 512])
        ps_tr = psum("ps_tr", [P, 512])
        ps_in = psum("ps_in", [P, 512])
        ps_h = psum("ps_h", [P, FC, P])
        ps_y = psum("ps_y", [P, 512])

        ident = cst[:, C_IDENT:C_IDENT + P]
        tri = cst[:, C_TRI:C_TRI + P]
        iota = cst[:, C_IOTA:C_IOTA + WIN]
        rank8 = cst[:, C_RANK:C_RANK + E8]

        def w1_at(b):
            return wsl[:, b, 0:KD * F].rearrange("p (k f) -> p k f", k=KD)

        def w2_at(b):
            return wsl[:, b, KD * F:KD * F + FC * D].rearrange("p (c d) -> p c d", c=FC)

        def b1_at(b):
            return wsl[:, b, KD * F + FC * D:KD * F + FC * D + FC]

        def b2_at(b):
            return wsl[:, b, WSZ - D:WSZ]

        ln_space = wsl[:, :, :].rearrange("p a b -> p (a b)")

        def ln_buf(u):
            return ln_space[:, u * LN_TILES * D:(u + 1) * LN_TILES * D].rearrange("p (t d) -> p t d", d=D)

        PLACES = [0, 1]

        def yg_at(place):
            return yg[:, :] if place == 0 else msg[:, place - 1, :]

        def xg_at(place):
            return xg[:, :] if place == 0 else msg[:, LATE_FINS + place - 1, :]

        ln_small = sb("ln_small", [P, LN_BUFS, LN_TILES, 10])
        msg_flat = msg[:, :, :].rearrange("p g d -> p (g d)")
        dst_i = msg_flat[:, 0:COLS].bitcast(I32)
        lim_sb = msg_flat[:, COLS:COLS + 3 * (NG + 1)]
        chk = msg_flat[:, COLS + 3 * (NG + 1):COLS + 6 * (NG + 1) + 8]

        s_const = sem("s_const")
        s_edges = sem("s_edges")
        s_memset = sem("s_memset")
        s_lnx = [sem(f"s_lnx{u}") for u in range(LN_BUFS)]
        s_lnmv = sem("s_lnmv")
        s_lnsd = sem("s_lnsd")
        s_lnrs = sem("s_lnrs")
        s_lny = sem("s_lny")
        s_lnyv = sem("s_lnyv")
        s_lnst = [sem(f"s_lnst{u}") for u in range(LN_BUFS)]
        s_lnc = sem("s_lnc")
        s_lnl = sem("s_lnl")
        s_pre = sem("s_pre")
        s_zero = sem("s_zero")
        s_prepe = sem("s_prepe")
        s_flag = sem("s_flag")
        g_idx, g_msg, g_onehot, g_mm, g_dve = (sem(q) for q in ("g_idx", "g_msg", "g_onehot", "g_mm", "g_dve"))
        s_idx = [sem(f"s_idx{q}") for q in range(3)]
        s_onehot = [sem(f"s_onehot{q}") for q in range(3)]
        s_msg = [sem(f"s_msg{q}") for q in range(3)]
        s_mm = [sem(f"s_mm{q}") for q in range(3)]
        s_added = [sem(f"s_added{q}") for q in range(3)]
        s_eq = sem("s_eq")
        s_aggS, s_n1, s_xt, s_x2, s_x2st = (sem(q) for q in ("s_aggS", "s_n1", "s_xt", "s_x2", "s_x2st"))
        s_nlink, s_mv, s_sd, s_h = (sem(q) for q in ("s_nlink", "s_mv", "s_sd", "s_h"))
        s_tr, s_hTs, s_log, s_ls, s_exp, s_choice, s_rank, s_route, s_scat = (
            sem(q) for q in ("s_tr", "s_hTs", "s_log", "s_ls", "s_exp", "s_choice", "s_rank", "s_route", "s_scat"))
        s_slink, s_plan, s_pad, s_dummy = (sem(q) for q in ("s_slink", "s_plan", "s_pad", "s_dummy"))
        s_hin = [sem(f"s_hin{b}") for b in range(2)]
        s_w = [sem(f"s_w{b}") for b in range(2)]
        s_yst = [sem(f"s_yst{b}") for b in range(2)]
        s_ft, s_hTf, s_l1, s_relu, s_l2, s_y = (sem(q) for q in ("s_ft", "s_hTf", "s_l1", "s_relu", "s_l2", "s_y"))
        s_yidx, s_fin, s_checked = (sem(q) for q in ("s_yidx", "s_fin", "s_checked"))
        s_yg = [sem(f"s_yg{b}") for b in range(1 + LATE_FINS)]
        s_xg = [sem(f"s_xg{b}") for b in range(1 + LATE_FINS)]
        s_out = [sem(f"s_out{b}") for b in range(1 + LATE_FINS)]
        s_redo, s_redope, s_again = (sem(q) for q in ("s_redo", "s_redope", "s_again"))
        r_idx, r_in, r_dve, r_out = (sem(q) for q in ("r_idx", "r_in", "r_dve", "r_out"))
        s_held = {q: sem("s_held_" + q) for q in ("sp", "act", "pe", "dve", "pool")}

        def finite_col(f, r):
            return finite[0:r, bass.ds(f, 1)]

        def known(value):
            return isinstance(value, int)

        def later(value):
            return not (known(value) and value == 0)

        def hold(eng, name, semaphore, value):
            eng.wait_ge(semaphore, value)
            if not known(value):
                eng.sem_inc(s_held[name], 1)

        class Links:

            def __init__(self, eng, name, semaphore, start):
                self.eng, self.name, self.semaphore, self.start, self.n = eng, name, semaphore, start, 0

            def mark(self, instruction):
                instruction.then_inc(self.semaphore, 1)
                self.n += 1

            def wait(self):
                hold(self.eng, self.name, self.semaphore, self.start + self.n)

            def __call__(self, instruction):
                self.mark(instruction)
                self.wait()

        @contextmanager
        def iterations(eng, count):
            if count == 1:
                yield 0
            else:
                with eng.Fori(0, count) as t:
                    yield t

        def walk(eng, steps, sched=None):
            used = {}
            for count, body, strides in TIMELINE:
                if "sched" in body[0]:
                    if sched:
                        sched(body[0]["sched"])
                    continue
                per_body = {}
                for it in body:
                    for j in range(it.get("fins", 0)):
                        place = PLACES[it["place"]] + j
                        per_body[place] = per_body.get(place, 0) + 1
                with iterations(eng, count) as t:
                    here = {}
                    for it in body:
                        at = {x: it[x] + t * strides.get(x, 0) if x in it else None for x in MOVING}
                        ffns = [(at["ffn"] + j, (it["ffn"] + j) % 2) for j in range(it.get("ffns", 0))]
                        fins = []
                        for j in range(it.get("fins", 0)):
                            place = PLACES[it["place"]] + j
                            before = used.get(place, 0) + here.get(place, 0)
                            fins.append((at["fin"] + j, place, before + t * per_body[place]))
                            here[place] = here.get(place, 0) + 1
                        steps(at["agg"], at["node"], ffns, fins, it)
                for place, n in per_body.items():
                    used[place] = used.get(place, 0) + n * count

        def all_stored(eng):
            for place in range(1 + LATE_FINS):
                n = sum(1 for it in STEPS for j in range(it.get("fins", 0)) if PLACES[it["place"]] + j == place)
                if n:
                    eng.wait_ge(s_out[place], 16 * n)
            eng.wait_ge(s_redo, 3)

        def each_row_tile(eng, step):
            step(0, P)
            with eng.Fori(1, NT - 1) as f:
                step(f, P)
            step(NT - 1, LAST_ROWS)

        def rows_of(n):
            return LAST_ROWS if known(n) and n == NT - 1 else P

        def of_parity(total, b):
            return (total + 1 - b) // 2

        def half(k, b):
            return (k - b) // 2

        def ln_stores(u):
            total = 16 * len([b for b in range(LN_FULL) if b % LN_BUFS == u])
            left = N - LN_FULL * LN_ROWS
            if u == LN_FULL % LN_BUFS:
                total += 16 * ((left // P > 0) + (left % P > 0))
            return total

        LN_TOTAL = LN_FULL + (N > LN_FULL * LN_ROWS)

        def ln_tiles(b):
            return LN_TILES if b < LN_FULL else -(-(N - LN_FULL * LN_ROWS) // P)

        def ln_rows(b, t):
            left = N - LN_FULL * LN_ROWS
            return left % P if known(b) and b == LN_FULL and t == left // P else P

        def ln_batches(eng, ahead, batch):
            total, tiles_of = LN_TOTAL, ln_tiles
            rounds = (total - 2) // LN_BUFS
            ahead(0, 0, tiles_of(0))
            if rounds > 0:
                with iterations(eng, rounds) as r:
                    for u in range(LN_BUFS):
                        ahead(r * LN_BUFS + u + 1, (u + 1) % LN_BUFS, LN_TILES)
                        batch(r * LN_BUFS + u, u, LN_TILES)
            for b in range(rounds * LN_BUFS, total):
                if b + 1 < total:
                    ahead(b + 1, (b + 1) % LN_BUFS, tiles_of(b + 1))
                batch(b, b % LN_BUFS, tiles_of(b))

        LINKS_NODE, LINKS_SCHED, LINKS_REDO = 19, 46, 7
        block = ctx.enter_context(nc.Block())

        @block.sync
        def _(sp):
            for dst, source in ((cst[:, :], consts), (wg_sb[:, :, :], w_gnn), (gw_sb[:, :, :], gate_w),
                                (bg_sb[:, :], b_gnn.partition_broadcast(P)),
                                (gb_sb[:, :], gate_b.partition_broadcast(P))):
                sp.dma_start(dst, source).then_inc(s_const, 16)
            for dst, source in ((dst_i, dst_t), (lim_sb, limits)):
                sp.dma_start(dst, source).then_inc(s_edges, 16)

            def load(b, u, again):
                if again is not None:
                    hold(sp, "sp", s_lnst[u], again)
                sp.dma_start(ln_buf(u), x[bass.ds(b * LN_ROWS, LN_ROWS), :].rearrange(
                    "(p t) d -> p t d", t=LN_TILES)).then_inc(s_lnx[u], 16)

            rounds = LN_FULL // LN_BUFS
            if rounds:
                for u in range(LN_BUFS):
                    load(u, u, None)
            for dst, source in ((src_sb[:, :], src_t), (wgt[:, :], w_t)):
                sp.dma_start(dst, source).then_inc(s_edges, 16)
            if rounds > 1:
                with sp.Fori(1, rounds) as r:
                    for u in range(LN_BUFS):
                        load(r * LN_BUFS + u, u, r * 16)
            for b in range(rounds * LN_BUFS, LN_FULL):
                load(b, b % LN_BUFS, 16 * (b // LN_BUFS))
            b, u = LN_FULL, LN_FULL % LN_BUFS
            left = N - LN_FULL * LN_ROWS
            if b >= LN_BUFS:
                hold(sp, "sp", s_lnst[u], 16 * (b // LN_BUFS))
            if left // P:
                sp.dma_start(ln_buf(u)[:, 0:left // P, :], x[b * LN_ROWS:b * LN_ROWS + left // P * P, :].rearrange(
                    "(p t) d -> p t d", t=left // P)).then_inc(s_lnx[u], 16)
            if left % P:
                sp.dma_start(ln_buf(u)[0:left % P, left // P, :], x[N - left % P:N, :]).then_inc(s_lnx[u], 16)
            for s in range(S):
                row = BASE[s] + E8 * CAPS[s]
                sp.dma_start(hbuf[row:row + P, :], zeros).then_inc(s_dummy, 16)
            for u in range(LN_BUFS):
                hold(sp, "sp", s_lnst[u], ln_stores(u))

            def steps(a, n, ffns, fins, it):
                for k, b in ffns:
                    expert = sp.value_load(plan[0:1, bass.ds(k * 4, 1)], min_val=0, max_val=E8 - 1)
                    first = sp.value_load(plan[0:1, bass.ds(k * 4 + 1, 1)], min_val=0, max_val=ROWS - P)
                    changed = sp.value_load(plan[0:1, bass.ds(k * 4 + 3, 1)], min_val=0, max_val=1)
                    expert, first = sp.snap(expert), sp.snap(first)
                    if not (known(k) and k < 2):
                        hold(sp, "sp", s_ft, k - 1)
                        hold(sp, "sp", s_y, k - 1)
                    sp.dma_start(hin[:, b, :], hbuf[bass.ds(first, P), :]).then_inc(s_hin[b], 16)
                    with sp.If(changed >= 1):
                        sp.dma_start(w1_at(b), w1[bass.ds(expert, 1)].rearrange(
                            "e p k f -> p (e k) f")).then_inc(s_w[b], 16)
                        sp.dma_start(w2_at(b), w2[bass.ds(expert, 1)].rearrange(
                            "e p c d -> p (e c) d")).then_inc(s_w[b], 16)
                        sp.dma_start(b1_at(b), b1[bass.ds(expert, 1)].rearrange(
                            "e p c -> p (e c)")).then_inc(s_w[b], 16)
                        sp.dma_start(b2_at(b), b2[bass.ds(expert, 1)].rearrange(
                            "e p d -> p (e d)")).then_inc(s_w[b], 16)
                    with sp.Else():
                        sp.sem_inc(s_w[b], 64)
                if n is not None:
                    if later(n):
                        hold(sp, "sp", s_x2st, n * 16)
                        hold(sp, "sp", s_h, n)
                    r = rows_of(n)
                    sp.dma_start(xt[0:r, :], x[bass.ds(n * P, r), :]).then_inc(s_xt, 16)
                    hold(sp, "sp", s_x2, n + 1)
                    sp.dma_start(x2_dram[bass.ds(n * P, r), :], xt[0:r, :]).then_inc(s_x2st, 16)
                for f, place, used in fins:
                    r = rows_of(f)
                    if later(used):
                        hold(sp, "sp", s_out[place], used * 16)
                    sp.dma_start(xg_at(place)[0:r, :], x2_dram[bass.ds(f * P, r), :]).then_inc(s_xg[place], 16)

            def sched(s):
                if s == S:
                    return
                hold(sp, "sp", s_plan, s + 1)
                hold(sp, "sp", s_x2st, 16 * sum(SEG[:s + 1]))
                for e in range(E8):
                    row = sp.value_load(pads[0:1, s * E8 + e:s * E8 + e + 1], min_val=0, max_val=ROWS - P)
                    sp.dma_start(hbuf[bass.ds(row, P), :], zeros).then_inc(s_pad, 16)
                sp.wait_ge(s_pad, 16 * E8 * (s + 1))
                sp.wait_ge(s_dummy, 16 * S)
                sp.wait_ge(s_scat, 16 * sum(SEG[:s + 1]))
                if s == S - 1:
                    for q in range(3):
                        sp.wait_ge(s_mm[q], NG)

            hold(sp, "sp", s_flag, 1)
            walk(sp, steps, sched)
            all_stored(sp)
            redo = sp.value_load(flag_i[0:1, 1:2], min_val=0, max_val=1)
            with sp.If(redo >= 1):
                def again(f, r):
                    if later(f):
                        hold(sp, "sp", r_out, f * 16)
                    sp.dma_start(xg_at(1)[0:r, :], x2_dram[bass.ds(f * P, r), :]).then_inc(r_in, 16)
                    hold(sp, "sp", r_dve, f * LINKS_REDO + LINKS_REDO)
                    sp.dma_start(out[bass.ds(f * P, r), :], xg_at(1)[0:r, :]).then_inc(r_out, 16)

                each_row_tile(sp, again)
                sp.wait_ge(r_out, 16 * NT)
            with sp.Else():
                sp.sem_inc(s_held["sp"], 1)

        @block.gpsimd
        def _(pool):
            pool.memset(aggT[:, :, :], 0.0).then_inc(s_zero, 1)
            for u in range(LN_BUFS):
                pool.wait_ge(s_lnst[u], ln_stores(u))
            pool.wait_ge(s_flag, 1)
            fast = pool.value_load(flag_i[0:1, 0:1], min_val=0, max_val=1)
            with pool.If(fast < 1):
                with pool.Fori(0, NG) as g:
                    hold(pool, "pool", g_idx, g + 1)
                    for j in range(G):
                        pool.indirect_dma_start(
                            out=msg[:, j, :], out_offset=None, in_=ln_dram,
                            in_offset=bass.IndirectOffsetOnAxis(ap=idx[:, j:j + 1], axis=0)).then_inc(g_msg, 16)
            with pool.Else():
                pool.sem_inc(s_held["pool"], 1)

            def gather(a, q):
                hold(pool, "pool", s_idx[q], a + 1)
                for j in range(OFF[q], OFF[q] + SUBS[q]):
                    pool.indirect_dma_start(
                        out=msg[:, j, :], out_offset=None, in_=ln_dram,
                        in_offset=bass.IndirectOffsetOnAxis(ap=idx[:, j:j + 1], axis=0)).then_inc(s_msg[q], 16)

            def steps(a, n, ffns, fins, it):
                if a is not None:
                    if known(a) and a == 0:
                        gather(a, 0)
                    gather(a, 1)
                    gather(a, 2)
                for f, place, used in fins:
                    r = rows_of(f)
                    hold(pool, "pool", s_yidx, f + 1)
                    if known(f):
                        outputs_of(1 if it["source"] == 0 else S if it["source"] == 2 else S - 1)
                    pool.indirect_dma_start(
                        out=yg_at(place)[0:r, :], out_offset=None, in_=ybuf[it["source"]],
                        in_offset=bass.IndirectOffsetOnAxis(ap=yidx[0:r, place:place + 1], axis=0)
                    ).then_inc(s_yg[place], 16)
                if a is not None and not (known(a) and a == NG - 1):
                    gather(a + 1, 0)
                if n is not None:
                    r = rows_of(n)
                    hold(pool, "pool", s_route, n + 1)
                    pool.indirect_dma_start(
                        out=hbuf, out_offset=bass.IndirectOffsetOnAxis(ap=slot_i[0:r, 0:1], axis=0),
                        in_=hrow[0:r, :], in_offset=None).then_inc(s_scat, 16)

            def outputs_of(segments):
                for q in range(2):
                    pool.wait_ge(s_yst[q], 16 * of_parity(sum(FFN[:segments]), q))

            def sched(s):
                if s >= S - 1:
                    outputs_of(s)
                if s == S - 1:
                    for q in range(3):
                        pool.wait_ge(s_mm[q], NG)

            walk(pool, steps, sched)
            all_stored(pool)
            redo = pool.value_load(flag_i[0:1, 1:2], min_val=0, max_val=1)
            with pool.If(redo >= 1):
                bounds = [0, SEG[0], sum(SEG[:-1]), NT]
                for g in range(3):
                    def again(f, r):
                        hold(pool, "pool", r_idx, f + 1)
                        pool.indirect_dma_start(
                            out=yg_at(1)[0:r, :], out_offset=None, in_=ybuf[g],
                            in_offset=bass.IndirectOffsetOnAxis(ap=yidx[0:r, 0:1], axis=0)).then_inc(r_in, 16)

                    end = min(bounds[g + 1], NT - 1)
                    if bounds[g] < end:
                        with pool.Fori(bounds[g], end) as f:
                            again(f, P)
                    if g == 2:
                        again(NT - 1, LAST_ROWS)
            with pool.Else():
                pool.sem_inc(s_held["pool"], 1)

        @block.scalar
        def _(act):
            act.wait_ge(s_memset, 2)

            def deviation(b, u, tiles):
                small = ln_small[:, u, 0:tiles, :]
                hold(act, "act", s_lnmv, b + 1)
                nc.scalar.activation(small[:, :, 8], small[:, :, 7], ACT.Sqrt, bias=eps[:, 0:1]).then_inc(s_lnsd, 1)

            def normalize(b, u, tiles):
                small = ln_small[:, u, 0:tiles, :]
                hold(act, "act", s_lnrs, b + 1)
                for t in range(min(tiles, LN_ON_ACT)):
                    r = ln_rows(b, t)
                    last = nc.scalar.activation(ln_buf(u)[0:r, t, :], ln_buf(u)[0:r, t, :], ACT.Identity,
                                                bias=small[0:r, t, 9:10], scale=small[0:r, t, 8:9])
                last.then_inc(s_lny, 1)
                hold(act, "act", s_lny, b + 1)
                hold(act, "act", s_lnyv, b + 1)
                if known(b) and b == LN_FULL:
                    left = N - LN_FULL * LN_ROWS
                    if left // P:
                        act.dma_start(ln_dram[b * LN_ROWS:b * LN_ROWS + left // P * P, :].rearrange(
                            "(p t) d -> p t d", t=left // P), ln_buf(u)[:, 0:left // P, :]).then_inc(s_lnst[u], 16)
                    if left % P:
                        act.dma_start(ln_dram[N - left % P:N, :], ln_buf(u)[0:left % P, left // P, :]
                                      ).then_inc(s_lnst[u], 16)
                else:
                    act.dma_start(ln_dram[bass.ds(b * LN_ROWS, LN_ROWS), :].rearrange(
                        "(p t) d -> p t d", t=LN_TILES), ln_buf(u)).then_inc(s_lnst[u], 16)

            ln_batches(act, deviation, normalize)

            def relu(k, b):
                hold(act, "act", s_w[b], half(k, b) * 64 + 64)
                for c in range(FC):
                    if c % HALF == 0:
                        hold(act, "act", s_l1, k * 2 + c // HALF + 1)
                    ins = nc.scalar.activation(hmid[:, c, :], ps_h[:, c, :], ACT.Relu, bias=b1_at(b)[:, c:c + 1])
                    if c % HALF == HALF - 1:
                        ins.then_inc(s_relu, 1)

            def steps(a, n, ffns, fins, it):
                if n is not None:
                    hold(act, "act", s_added[2], min(n + LAG, NG) if known(n) else n + LAG)
                    if later(n):
                        hold(act, "act", s_n1, n)
                    nc.scalar.copy(aggS[:, :, :], aggT[:, :, bass.ds(n * P, P)]).then_inc(s_aggS, 1)
                    hold(act, "act", s_mv, n + 1)
                    nc.scalar.activation(sd[:, :], mv[:, 1:2], ACT.Sqrt, bias=eps[:, 0:1]).then_inc(s_sd, 1)
                if ffns:
                    relu(*ffns[0])
                if n is not None:
                    hold(act, "act", s_tr, n + 1)
                    if later(n):
                        hold(act, "act", s_log, n)
                    nc.scalar.copy(hTs[:, :, :], ps_tr[:, 0:D].rearrange("p (k t) -> p k t", k=KD)
                                   ).then_inc(s_hTs, 1)
                    hold(act, "act", s_ls, n + 1)
                    nc.scalar.activation(rt[:, 2 * E8:3 * E8], rt[:, E8:2 * E8], ACT.Exp,
                                         accum_out=sc[:, 1:2]).then_inc(s_exp, 1)
                if len(ffns) > 1:
                    relu(*ffns[1])
                for k, b in ffns:
                    hold(act, "act", s_y, k + 1)
                    act.dma_start(ybuf[it["to"]][bass.ds((k - KBUF[it["to"]]) * P, P), :], yrow[:, b, :]
                                  ).then_inc(s_yst[b], 16)
                for f, place, used in fins:
                    r = rows_of(f)
                    hold(act, "act", s_fin, f + 1)
                    nc.scalar.activation(junk[0:r, :], xg_at(place)[0:r, :], ACT.Copy, scale=0.0,
                                         accum_out=finite_col(f, r)).then_inc(s_checked, 1)
                    hold(act, "act", s_checked, f + 1)
                    act.dma_start(out[bass.ds(f * P, r), :], xg_at(place)[0:r, :]).then_inc(s_out[place], 16)

            walk(act, steps)

        @block.tensor
        def _(pe):
            pe.wait_ge(s_const, 80)
            pe.wait_ge(s_memset, 2)
            pe.wait_ge(s_pre, 1)
            for q in range(3):
                firsts = rel[0:1, OFF[q]:OFF[q] + NG * G + 1:G]
                last = nc.tensor.matmul(ps_h[:, q, 0:NG + 1], ones[0:1, :], firsts, start=True, stop=True)
            last.then_inc(s_prepe, 1)
            pe.wait_ge(s_pre, 2)
            nc.tensor.transpose(ps_tr[0:1, 0:P], chk[:, 0:1], ident).then_inc(s_prepe, 1)
            pe.wait_ge(s_pre, 3)
            nc.tensor.matmul(ps_tr[:, P:P + 1], ones[0:1, :], chk[0:1, 2:3], start=True, stop=True
                             ).then_inc(s_prepe, 1)

            pe.wait_ge(s_flag, 1)
            fast = pe.value_load(flag_i[0:1, 0:1], min_val=0, max_val=1)
            with pe.If(fast < 1):
                with pe.Fori(0, NG) as g:
                    hold(pe, "pe", g_msg, g * (16 * G) + 16 * G)
                    with pe.Fori(0, WINDOWS) as w:
                        hold(pe, "pe", g_onehot, g * WINDOWS + w + 1)
                        for k in range(KD):
                            for j in range(G):
                                last = nc.tensor.matmul(ps_agg[:, 0, k * WIN:(k + 1) * WIN],
                                                        msg[:, j, k * P:(k + 1) * P], onehot[:, j, :],
                                                        start=j == 0, stop=j == G - 1)
                        last.then_inc(g_mm, 1)
            with pe.Else():
                pe.sem_inc(s_held["pe"], 1)

            def sub(a, q):
                hold(pe, "pe", s_msg[q], a * (16 * SUBS[q]) + 16 * SUBS[q])
                hold(pe, "pe", s_onehot[q], a + 1)
                if q == 2:
                    hold(pe, "pe", s_added[0], a + 1)
                elif later(a):
                    hold(pe, "pe", s_added[2 - q], a)
                for k in range(KD):
                    for j in range(OFF[q], OFF[q] + SUBS[q]):
                        last = nc.tensor.matmul(ps_agg[:, q % 2, k * WIN:(k + 1) * WIN],
                                                msg[:, j, k * P:(k + 1) * P], onehot[:, j, :],
                                                start=j == OFF[q], stop=j == OFF[q] + SUBS[q] - 1)
                last.then_inc(s_mm[q], 1)

            def gnn(n):
                hold(pe, "pe", s_aggS, n + 1)
                if later(n):
                    hold(pe, "pe", s_x2, n)
                for k in range(KD):
                    last = nc.tensor.matmul(ps_x2[:, 0:D], aggS[:, k, :], wg_sb[:, k, :],
                                            start=k == 0, stop=k == KD - 1)
                last.then_inc(s_n1, 1)

            def turn_node(n):
                hold(pe, "pe", s_h, n + 1)
                if later(n):
                    hold(pe, "pe", s_route, n)
                for k in range(KD):
                    last = nc.tensor.transpose(ps_tr[:, k * P:(k + 1) * P], hrow[:, k * P:(k + 1) * P], ident)
                last.then_inc(s_tr, 1)

            def logits(n):
                hold(pe, "pe", s_hTs, n + 1)
                for k in range(KD):
                    last = nc.tensor.matmul(ps_tr[:, D:D + E8], hTs[:, k, :], gw_sb[:, k, :],
                                            start=k == 0, stop=k == KD - 1)
                last.then_inc(s_log, 1)

            def ranks(n):
                r = rows_of(n)
                hold(pe, "pe", s_choice, n + 1)
                choice = rt[0:r, 3 * E8:4 * E8]
                nc.tensor.matmul(ps_tr[:, D + E8:D + 2 * E8], tri[0:r, :], choice, start=True, stop=True)
                nc.tensor.matmul(ps_tr[:, D + 2 * E8:D + 3 * E8], ones[0:r, :], choice, start=True, stop=True
                                 ).then_inc(s_rank, 1)

            def turn_ffn(k, b):
                hold(pe, "pe", s_hin[b], half(k, b) * 16 + 16)
                if not (known(k) and k == 0):
                    hold(pe, "pe", s_hTf, k)
                for q in range(KD):
                    last = nc.tensor.transpose(ps_in[:, q * P:(q + 1) * P], hin[:, b, q * P:(q + 1) * P], ident)
                last.then_inc(s_ft, 1)

            def layer1(k, b):
                hold(pe, "pe", s_hTf, k + 1)
                hold(pe, "pe", s_w[b], half(k, b) * 64 + 64)
                for c in range(FC):
                    for q in range(KD):
                        last = nc.tensor.matmul(ps_h[:, c, :], w1_at(b)[:, q, c * P:(c + 1) * P], hTf[:, q, :],
                                                start=q == 0, stop=q == KD - 1)
                    if c % HALF == HALF - 1:
                        last.then_inc(s_l1, 1)

            def layer2(k, b):
                if later(k):
                    hold(pe, "pe", s_y, k)
                for c in range(FC):
                    if c % HALF == 0:
                        hold(pe, "pe", s_relu, k * 2 + c // HALF + 1)
                    last = nc.tensor.matmul(ps_y[:, 0:D], hmid[:, c, :], w2_at(b)[:, c, :],
                                            start=c == 0, stop=c == FC - 1)
                last.then_inc(s_l2, 1)

            def steps(a, n, ffns, fins, it):
                if ffns:
                    turn_ffn(*ffns[0])
                if n is not None:
                    gnn(n)
                if ffns:
                    layer1(*ffns[0])
                if n is not None:
                    turn_node(n)
                if ffns:
                    layer2(*ffns[0])
                if n is not None:
                    logits(n)
                if len(ffns) > 1:
                    turn_ffn(*ffns[1])
                if a is not None:
                    sub(a, 0)
                if len(ffns) > 1:
                    layer1(*ffns[1])
                if n is not None:
                    ranks(n)
                if a is not None:
                    sub(a, 1)
                if len(ffns) > 1:
                    layer2(*ffns[1])
                if a is not None:
                    sub(a, 2)

            walk(pe, steps)
            pe.wait_ge(s_redo, 1)
            nc.tensor.transpose(ps_tr[0:1, 0:P], fix[:, 0:1], ident).then_inc(s_redope, 1)

        @block.vector
        def _(dve):
            dve.memset(ones[:, :], 1.0).then_inc(s_memset, 1)
            dve.memset(eps[:, :], EPS).then_inc(s_memset, 1)
            dve.wait_ge(s_memset, 2)

            def moments(b, u, tiles):
                small = ln_small[:, u, 0:tiles, :]
                hold(dve, "dve", s_lnx[u], ln_stores(u) if known(b) and b == LN_FULL
                     else b // LN_BUFS * 16 + 16 if known(b) else (b - u) * (16 // LN_BUFS) + 16)
                for t in range(tiles):
                    r = ln_rows(b, t)
                    last = dve.bn_stats(small[0:r, t, 0:6], ln_buf(u)[0:r, t, :])
                last.then_inc(s_lnc, 1)
                hold(dve, "dve", s_lnc, b + 1)
                for t in range(tiles):
                    r = ln_rows(b, t)
                    last = dve.bn_aggr(small[0:r, t, 6:8], small[0:r, t, 0:6])
                last.then_inc(s_lnmv, 1)

            def scales(b, u, tiles):
                link = Links(dve, "dve", s_lnl, b * 2)
                small = ln_small[:, u, 0:tiles, :]
                hold(dve, "dve", s_lnsd, b + 1)
                link(dve.reciprocal(small[:, :, 8], small[:, :, 8]))
                link(dve.scalar_tensor_tensor(out=small[:, :, 9], in0=small[:, :, 6], scalar=-1.0,
                                              in1=small[:, :, 8], op0=ALU.mult, op1=ALU.mult))
                dve.sem_inc(s_lnrs, 1)
                for t in range(LN_ON_ACT, tiles):
                    r = ln_rows(b, t)
                    last = dve.tensor_scalar(ln_buf(u)[0:r, t, :], ln_buf(u)[0:r, t, :], small[0:r, t, 6:7],
                                             small[0:r, t, 8:9], ALU.subtract, ALU.mult)
                if tiles > LN_ON_ACT:
                    last.then_inc(s_lnyv, 1)
                else:
                    dve.sem_inc(s_lnyv, 1)

            dve.memset(ln_small[:, :, :, :], 0.0).then_inc(s_memset, 1)
            dve.wait_ge(s_memset, 3)

            link = Links(dve, "dve", sem("s_prelink"), 0)
            dve.wait_ge(s_const, 80)
            dve.wait_ge(s_edges, 64)
            link(dve.tensor_copy(rel[:, :], dst_i))
            dve.sem_inc(s_pre, 1)
            dve.wait_ge(s_prepe, 1)
            firsts = base_bc[:, :].rearrange("p (g q) -> p g q", q=3)
            for q in range(3):
                link.mark(dve.tensor_copy(firsts[:, :, q], ps_h[:, q, 0:NG + 1]))
            link.wait()
            link.mark(dve.tensor_copy(base_i[0:1, :], base_bc[0:1, :]))
            rel3 = rel[:, :].rearrange("p (g j) -> p g j", j=G)
            for q in range(3):
                part = rel3[:, :, OFF[q]:OFF[q] + SUBS[q]]
                link.mark(dve.tensor_tensor(part, part, firsts[:, :, q:q + 1].to_broadcast([P, NG + 1, SUBS[q]]),
                                            ALU.subtract))
            link(dve.tensor_tensor(chk[:, 8:8 + 3 * (NG + 1)], base_bc[:, :], lim_sb, ALU.subtract))
            link.mark(dve.tensor_reduce(chk[:, 3:4], rel[:, :], AX_X, ALU.min))
            link.mark(dve.tensor_reduce(chk[:, 4:5], rel[:, :], AX_X, ALU.max))
            link(dve.tensor_reduce(chk[:, 5:6], chk[:, 8:8 + 3 * (NG + 1)], AX_X, ALU.min))
            link(dve.tensor_scalar(chk[:, 4:5], chk[:, 4:5], -1.0, float(WIN - 1), ALU.mult, ALU.add))
            link(dve.tensor_tensor(chk[:, 3:4], chk[:, 3:4], chk[:, 4:5], ALU.min))
            link(dve.tensor_tensor(chk[:, 0:1], chk[:, 3:4], chk[:, 5:6], ALU.min))
            dve.sem_inc(s_pre, 1)
            dve.wait_ge(s_prepe, 2)
            link(dve.tensor_reduce(chk[0:1, 1:2], ps_tr[0:1, 0:P], AX_X, ALU.min))
            link(dve.tensor_scalar(chk[0:1, 2:3], chk[0:1, 1:2], 0.0, None, ALU.is_ge))
            dve.sem_inc(s_pre, 1)
            link.mark(dve.tensor_copy(flag_i[0:1, 0:1], chk[0:1, 2:3]))
            dve.wait_ge(s_prepe, 3)
            link.mark(dve.tensor_copy(flag_bc[:, :], ps_tr[:, P:P + 1]))
            link.mark(dve.memset(seen[:, :], 0.0))
            link.mark(dve.memset(hrow[:, :], 0.0))
            link.mark(dve.memset(xt[:, :], 0.0))
            link.mark(dve.tensor_copy(offs[:, :], cst[:, C_SEG:C_SEG + E8]))
            link.mark(dve.memset(finite[:, :], 0.0))
            link.wait()

            def nothing(b, u, tiles):
                if known(b) and b == 0:
                    moments(b, u, tiles)

            def scales_and_next(b, u, tiles):
                scales(b, u, tiles)
                if known(b):
                    if b < LN_TOTAL - 1:
                        moments(b + 1, (u + 1) % LN_BUFS, ln_tiles(b + 1))
                else:
                    moments(b + 1, (u + 1) % LN_BUFS, LN_TILES)

            ln_batches(dve, nothing, scales_and_next)
            dve.sem_inc(s_flag, 1)
            dve.wait_ge(s_zero, 1)

            fast = dve.value_load(flag_i[0:1, 0:1], min_val=0, max_val=1)
            with dve.If(fast < 1):
                at = fix[:, 0:G]
                with dve.Fori(0, NG) as g:
                    glink = Links(dve, "dve", g_dve, g * (5 + 4 * WINDOWS))
                    glink(dve.tensor_copy(idx[:, :], src_sb[:, bass.ds(g * G, G)]))
                    dve.sem_inc(g_idx, 1)
                    for q in range(3):
                        glink.mark(dve.tensor_tensor(
                            at[:, OFF[q]:OFF[q] + SUBS[q]], rel[:, bass.ds(g * G + OFF[q], SUBS[q])],
                            base_bc[:, bass.ds(g * 3 + q, 1)].to_broadcast([P, SUBS[q]]), ALU.add))
                    glink(dve.tensor_copy(fix[:, 32:32 + G], wgt[:, bass.ds(g * G, G)]))
                    with dve.Fori(0, WINDOWS) as w:
                        wlink = Links(dve, "dve", g_dve, g * (5 + 4 * WINDOWS) + w * 4 + 5)
                        wlink(dve.tensor_tensor(
                            onehot[:, :, :], iota.unsqueeze(1).to_broadcast([P, G, WIN]),
                            at.unsqueeze(2).to_broadcast([P, G, WIN]), ALU.is_equal))
                        wlink(dve.tensor_tensor(
                            onehot[:, :, :], onehot[:, :, :],
                            fix[:, 32:32 + G].unsqueeze(2).to_broadcast([P, G, WIN]), ALU.mult))
                        dve.sem_inc(g_onehot, 1)
                        hold(dve, "dve", g_mm, g * WINDOWS + w + 1)
                        columns = aggT[:, :, bass.ds(w * WIN, WIN)]
                        wlink(dve.tensor_tensor(
                            columns, columns, ps_agg[:, 0, 0:KD * WIN].rearrange("p (k c) -> p k c", k=KD), ALU.add))
                        wlink(dve.tensor_scalar(at, at, -float(WIN), None, ALU.add))
            with dve.Else():
                dve.sem_inc(s_held["dve"], 1)
            dve.tensor_scalar(wgt[:, :], wgt[:, :], flag_bc[:, 0:1], None, ALU.mult).then_inc(s_flag, 1)
            dve.wait_ge(s_flag, 2)

            def prep(a, q):
                n = SUBS[q]
                col = a * G + OFF[q]
                dve.tensor_copy(idx[:, OFF[q]:OFF[q] + n], src_sb[:, bass.ds(col, n)]).then_inc(s_idx[q], 1)
                hot = onehot[:, OFF[q]:OFF[q] + n, :]
                dve.tensor_tensor(hot, iota.unsqueeze(1).to_broadcast([P, n, WIN]),
                                  rel[:, bass.ds(col, n)].unsqueeze(2).to_broadcast([P, n, WIN]), ALU.is_equal
                                  ).then_inc(s_eq, 1)
                hold(dve, "dve", s_eq, a * 3 + q + 1)
                dve.tensor_tensor(hot, hot, wgt[:, bass.ds(col, n)].unsqueeze(2).to_broadcast([P, n, WIN]),
                                  ALU.mult).then_inc(s_onehot[q], 1)

            def sub(a, q):
                first = dve.snap(dve.value_load(base_i[0:1, bass.ds(a * 3 + q, 1)], min_val=0, max_val=N - 1))
                hold(dve, "dve", s_mm[q], a + 1)
                prev, val = (2, a) if q == 0 else (q - 1, a + 1)
                if not (known(a) and a == 0 and q == 0):
                    hold(dve, "dve", s_added[prev], val)
                columns = aggT[:, :, bass.ds(first, WIN)]
                dve.tensor_tensor(columns, columns, ps_agg[:, q % 2, 0:KD * WIN].rearrange("p (k c) -> p k c", k=KD), ALU.add
                                  ).then_inc(s_added[q], 1)
                prep(a + 1, q)

            def norm_a(n, link):
                hold(dve, "dve", s_xt, n * 16 + 16)
                link(dve.tensor_tensor(xt[:, :], xt[:, :], bg_sb[:, :], ALU.add))
                hold(dve, "dve", s_n1, n + 1)
                link.mark(dve.tensor_tensor(xt[:, :], xt[:, :], ps_x2[:, 0:D], ALU.add))
                link.wait()
                dve.sem_inc(s_x2, 1)
                link(dve.bn_stats(st6[:, :], xt[:, :]))
                link(dve.bn_aggr(mv[:, :], st6[:, :]))
                dve.sem_inc(s_mv, 1)

            def norm_b(n, link):
                hold(dve, "dve", s_sd, n + 1)
                link(dve.reciprocal(rs[:, :], sd[:, :]))
                if later(n):
                    hold(dve, "dve", s_scat, n * 16)
                dve.tensor_scalar(hrow[:, :], xt[:, :], mv[:, 0:1], rs[:, 0:1], ALU.subtract, ALU.mult
                                  ).then_inc(s_h, 1)

            def cols8(j):
                return rt[:, j * E8:(j + 1) * E8]

            def route_a(n, link):
                hold(dve, "dve", s_log, n + 1)
                link(dve.tensor_tensor(cols8(0), ps_tr[:, D:D + E8], gb_sb[:, :], ALU.add))
                link(dve.tensor_reduce(sc[:, 0:1], cols8(0), AX_X, ALU.max))
                link.mark(dve.tensor_scalar(cols8(1), cols8(0), sc[:, 0:1], None, ALU.subtract))
                link(dve.scalar_tensor_tensor(out=cols8(4), in0=cols8(0), scalar=sc[:, 0:1], in1=rank8,
                                              op0=ALU.is_ge, op1=ALU.mult))
                dve.sem_inc(s_ls, 1)
                link(dve.tensor_reduce(sc[:, 2:3], cols8(4), AX_X, ALU.max))
                link(dve.tensor_scalar(cols8(3), rank8, sc[:, 2:3], None, ALU.is_equal))
                dve.sem_inc(s_choice, 1)

            def route_b(n, link):
                hold(dve, "dve", s_rank, n + 1)
                hold(dve, "dve", s_exp, n + 1)
                link(dve.tensor_tensor(cols8(5), ps_tr[:, D + E8:D + 2 * E8], seen[:, :], ALU.add))
                link.mark(dve.tensor_tensor(seen[:, :], seen[:, :], ps_tr[:, D + 2 * E8:D + 3 * E8], ALU.add))
                link.mark(dve.tensor_tensor(cols8(6), cols8(5), cols8(3), ALU.mult))
                link.mark(dve.reciprocal(sc[:, 3:4], sc[:, 1:2]))
                link(dve.tensor_tensor(cols8(5), cols8(5), offs[:, :], ALU.add))
                link.mark(dve.tensor_reduce(sc[:, 4:5], cols8(6), AX_X, ALU.add))
                link(dve.tensor_tensor(cols8(7), cols8(5), cols8(3), ALU.mult))
                link(dve.tensor_reduce(sc[:, 5:6], cols8(7), AX_X, ALU.add))
                dve.scalar_tensor_tensor(out=gain[:, bass.ds(n, 1)], in0=sc[:, 4:5], scalar=float(CAP),
                                         in1=sc[:, 3:4], op0=ALU.is_lt, op1=ALU.mult)
                dve.tensor_copy(slots[:, bass.ds(n, 1)], sc[:, 5:6])
                dve.tensor_copy(chosen[:, bass.ds(n, 1)], sc[:, 2:3])
                dve.tensor_copy(slot_i[:, :], sc[:, 5:6]).then_inc(s_route, 1)

            def copy_in(k):
                hold(dve, "dve", s_ft, k + 1)
                if not (known(k) and k == 0):
                    hold(dve, "dve", s_l1, k * 2)
                dve.tensor_copy(hTf[:, :, :], ps_in[:, 0:D].rearrange("p (k t) -> p k t", k=KD)).then_inc(s_hTf, 1)

            def expert_out(k, b):
                hold(dve, "dve", s_l2, k + 1)
                if not (known(k) and k < 2):
                    hold(dve, "dve", s_yst[b], half(k, b) * 16)
                dve.tensor_tensor(yrow[:, b, :], ps_y[:, 0:D], b2_at(b), ALU.add).then_inc(s_y, 1)

            def final_index(f, place, used):
                if later(used):
                    hold(dve, "dve", s_yg[place], used * 16)
                dve.tensor_copy(yidx[:, place:place + 1], slots[:, bass.ds(f, 1)]).then_inc(s_yidx, 1)

            def final(f, place, used):
                r = rows_of(f)
                hold(dve, "dve", s_yg[place], used * 16 + 16)
                hold(dve, "dve", s_xg[place], used * 16 + 16)
                dve.scalar_tensor_tensor(out=xg_at(place)[0:r, :], in0=yg_at(place)[0:r, :],
                                         scalar=gain[0:r, bass.ds(f, 1)], in1=xg_at(place)[0:r, :],
                                         op0=ALU.mult, op1=ALU.add).then_inc(s_fin, 1)

            def steps(a, n, ffns, fins, it):
                link = Links(dve, "dve", s_nlink, n * LINKS_NODE) if n is not None else None
                for fin in fins:
                    final_index(*fin)
                if ffns:
                    copy_in(ffns[0][0])
                if n is not None:
                    norm_a(n, link)
                    norm_b(n, link)
                if ffns:
                    expert_out(*ffns[0])
                if n is not None:
                    route_a(n, link)
                if len(ffns) > 1:
                    copy_in(ffns[1][0])
                if a is not None:
                    sub(a, 0)
                if n is not None:
                    route_b(n, link)
                    assert link.n == LINKS_NODE, link.n
                if a is not None:
                    sub(a, 1)
                if len(ffns) > 1:
                    expert_out(*ffns[1])
                if a is not None:
                    sub(a, 2)
                for fin in fins:
                    final(*fin)

            def sched(s):
                if s == S:
                    return
                T, K, k0 = SEG[s], FFN[s], sum(FFN[:s])
                link = Links(dve, "dve", s_slink, s * LINKS_SCHED)
                io = iota[:, :]
                rows, n8, nt, cum, shift = (fix2[:, j * 8:(j + 1) * 8] for j in range(5))
                ek, stk = (fix2[:, 64 + j * 64:64 + j * 64 + K] for j in range(2))
                segrow = cst[:, C_SEG + s * E8:C_SEG + (s + 1) * E8]
                dve.wait_ge(s_route, sum(SEG[:s + 1]))
                link(dve.tensor_tensor(rows, seen[:, :], offs[:, :], ALU.add))
                link.mark(dve.tensor_copy(pads[0:1, s * E8:(s + 1) * E8], rows[0:1, :]))
                link(dve.tensor_tensor(n8, rows, segrow, ALU.subtract))
                link(dve.tensor_scalar(n8, n8, 1.0 / P, None, ALU.mult))
                cmp = fix[:, 0:E8 * (T + 1)].rearrange("p (e q) -> p e q", e=E8)
                link(dve.tensor_tensor(cmp, io[:, 0:T + 1].unsqueeze(1).to_broadcast([P, E8, T + 1]),
                                       n8.unsqueeze(2).to_broadcast([P, E8, T + 1]), ALU.is_lt))
                link(dve.tensor_reduce(nt, cmp, AX_X, ALU.add))
                link(dve.tensor_copy(cum, nt))
                for e in range(1, E8):
                    link(dve.tensor_tensor(cum[:, e:e + 1], cum[:, e:e + 1], cum[:, e - 1:e], ALU.add))
                past = fix[:, 0:K * E8].rearrange("p (k e) -> p k e", e=E8)
                link(dve.tensor_tensor(past, cum.unsqueeze(1).to_broadcast([P, K, E8]),
                                       io[:, 0:K].unsqueeze(2).to_broadcast([P, K, E8]), ALU.is_le))
                link(dve.tensor_reduce(ek, past, AX_X, ALU.add))
                link(dve.tensor_tensor(past, past, nt.unsqueeze(1).to_broadcast([P, K, E8]), ALU.mult))
                link(dve.tensor_reduce(stk, past, AX_X, ALU.add))
                link(dve.tensor_tensor(stk, io[:, 0:K], stk, ALU.subtract))
                link(dve.tensor_scalar(stk, stk, float(P), float(BASE[s]), ALU.mult, ALU.add))
                link(dve.scalar_tensor_tensor(out=stk, in0=ek, scalar=float(CAPS[s]), in1=stk,
                                              op0=ALU.mult, op1=ALU.add))
                rows4 = plan[0:1, 4 * k0:4 * (k0 + K)].rearrange("p (k c) -> p k c", c=4)
                link.mark(dve.tensor_scalar(rows4[:, :, 1], stk[0:1, :], float(BASE[s] + E8 * CAPS[s]), None, ALU.min))
                link(dve.tensor_scalar(ek, ek, float(E8 - 1), None, ALU.min))
                link.mark(dve.tensor_copy(rows4[:, :, 0], ek[0:1, :]))
                link.mark(dve.memset(rows4[:, 0:2, 3], 1))
                link(dve.tensor_tensor(rows4[:, 2:K, 3], ek[0:1, 2:K], ek[0:1, 0:K - 2], ALU.not_equal))
                dve.sem_inc(s_plan, 1)
                link(dve.tensor_tensor(shift, cum, nt, ALU.subtract))
                link(dve.tensor_scalar(shift, shift, float(P), float(P * (k0 - KBUF[buffer_of(s, S - 1)])),
                                       ALU.mult, ALU.add))
                link(dve.tensor_tensor(shift, shift, segrow, ALU.subtract))
                n0 = sum(SEG[:s])
                part, its = slots[:, n0:n0 + T], fix[:, 0:T]
                for e in range(E8):
                    link(dve.tensor_scalar(its, chosen[:, n0:n0 + T], float(E8 - e), shift[:, e:e + 1],
                                           ALU.is_equal, ALU.mult))
                    link(dve.tensor_tensor(part, part, its, ALU.add))
                assert link.n == LINKS_SCHED - 1, link.n
                if s + 1 < S:
                    link(dve.tensor_tensor(offs[:, :], cst[:, C_SEG + (s + 1) * E8:C_SEG + (s + 2) * E8],
                                           seen[:, :], ALU.subtract))

            for q in range(3):
                prep(0, q)
            walk(dve, steps, sched)

            dve.wait_ge(s_checked, NT)
            end = Links(dve, "dve", s_again, 0)
            end(dve.tensor_scalar(fix[:, 32:32 + NT], finite[:, :], 0.0, None, ALU.is_equal))
            end(dve.tensor_reduce(fix[:, 0:1], fix[:, 32:32 + NT], AX_X, ALU.min))
            dve.sem_inc(s_redo, 1)
            dve.wait_ge(s_redope, 1)
            end(dve.tensor_reduce(fix[0:1, 1:2], ps_tr[0:1, 0:P], AX_X, ALU.min))
            end(dve.tensor_scalar(flag_i[0:1, 1:2], fix[0:1, 1:2], 1.0, None, ALU.is_lt))
            dve.sem_inc(s_redo, 2)
            all_stored(dve)
            redo = dve.value_load(flag_i[0:1, 1:2], min_val=0, max_val=1)
            with dve.If(redo >= 1):
                def again(f, r):
                    fix_link = Links(dve, "dve", r_dve, f * LINKS_REDO)
                    y, x2 = yg_at(1)[0:r, :], xg_at(1)[0:r, :]
                    kept, low, high = (msg[0:r, 2 * LATE_FINS + q, :] for q in range(3))
                    dve.tensor_copy(yidx[:, 0:1], slots[:, bass.ds(f, 1)]).then_inc(r_idx, 1)
                    hold(dve, "dve", r_in, f * 32 + 32)
                    fix_link(dve.tensor_scalar(y, y, gain[0:r, bass.ds(f, 1)], None, ALU.mult))
                    fix_link.mark(dve.tensor_scalar(low, y, -FLT_MAX, -1e4, ALU.is_lt, ALU.mult))
                    fix_link.mark(dve.tensor_scalar(kept.bitcast(I32), y, 0.0, 0.0, ALU.mult, ALU.is_equal))
                    fix_link(dve.tensor_scalar(high, y, FLT_MAX, 1e4, ALU.is_gt, ALU.mult))
                    fix_link(dve.tensor_tensor(low, low, high, ALU.add))
                    fix_link(dve.copy_predicated(low, kept.bitcast(I32), y))
                    fix_link(dve.tensor_tensor(x2, x2, low, ALU.add))
                    assert fix_link.n == LINKS_REDO

                each_row_tile(dve, again)
            with dve.Else():
                dve.sem_inc(s_held["dve"], 1)


def kernel(**inputs):
    import numpy as np
    import concourse.bacc as bacc
    from concourse.bass_utils import run_bass_kernel_spmd

    x = np.ascontiguousarray(inputs["x"])
    N, D = x.shape
    edges = inputs["src"].shape[0]
    experts = inputs["L0_ffn_gate_w"].shape[1]
    F = inputs["L0_ffn_b1"].shape[1]
    z = layout_of(N, edges, experts)
    NT, COLS, S = z["tiles"], z["columns"], len(z["seg"])

    def by_tile(a, fill):
        a = np.asarray(a)
        whole = np.full(COLS * P, fill, a.dtype)
        whole[:edges] = a
        return np.ascontiguousarray(whole.reshape(COLS, P).T)

    consts = np.zeros((P, C_SEG + experts * S), np.float32)
    consts[:, C_IDENT:C_IDENT + P] = np.eye(P)
    consts[:, C_TRI:C_TRI + P] = np.triu(np.ones((P, P)), 1)
    consts[:, C_IOTA:C_IOTA + WIN] = np.arange(WIN)
    consts[:, C_RANK:C_RANK + experts] = experts - np.arange(experts)
    for s in range(S):
        consts[:, C_SEG + s * experts:C_SEG + (s + 1) * experts] = z["base"][s] + z["caps"][s] * np.arange(experts)
    limits = np.broadcast_to(np.repeat(P * (np.arange(NT + 1) - 1), 3).astype(np.float32), (P, 3 * (NT + 1)))

    def rows(a, chunk):
        a = np.asarray(a)
        *lead, r, c = a.shape
        return np.ascontiguousarray(np.moveaxis(a.reshape(*lead, r // P, P, c), -3, -2))

    arrays = dict(
        x=x, src_t=by_tile(inputs["src"], 0), dst_t=by_tile(inputs["dst"], N - 1),
        w_t=by_tile(inputs["edge_weight"], 0),
        w_gnn=rows(np.asarray(inputs["L0_gnn_W"]).T, P), b_gnn=np.asarray(inputs["L0_gnn_b"]).reshape(1, D),
        gate_w=rows(inputs["L0_ffn_gate_w"], P), gate_b=np.asarray(inputs["L0_ffn_gate_b"]),
        w1=rows(inputs["L0_ffn_w1"], P),
        b1=np.ascontiguousarray(np.asarray(inputs["L0_ffn_b1"]).reshape(experts, F // P, P).transpose(0, 2, 1)),
        w2=rows(inputs["L0_ffn_w2"], P),
        b2=np.ascontiguousarray(np.broadcast_to(np.asarray(inputs["L0_ffn_b2"])[:, None, :], (experts, P, D))),
        consts=consts, limits=np.ascontiguousarray(limits), zeros=np.zeros((P, D), np.float32),
    )
    nc = bacc.Bacc("TRN2", target_bir_lowering=False, num_devices=1)
    args = {name: nc.dram_tensor(f"in_{name}", a.shape, mybir.dt.from_np(a.dtype), kind="ExternalInput").ap()
            for name, a in arrays.items()}
    out = nc.dram_tensor("out_x", (N, D), F32, kind="ExternalOutput").ap()
    gnn_moe_kernel(nc, *args.values(), out, z)
    r = run_bass_kernel_spmd(nc, [{f"in_{name}": a for name, a in arrays.items()}], core_ids=[0])
    return r.results[0]["out_x"]
```

```python
from contextlib import ExitStack, contextmanager

import concourse.bass as bass
from concourse import mybir

P = 128
ALU = mybir.AluOpType
ACT = mybir.ActivationFunctionType
F32 = mybir.dt.float32
I32 = mybir.dt.int32
AX_X = mybir.AxisListType.X

WIN = 64
LAG = 2
CAPACITY_FACTOR = 1.25
EPS = 1e-5
FLT_MAX = 3.4028234663852886e38
EXTRA = 2
LN_TILES = 7
LN_BUFS = 4
MOST_FINS = 6
C_IDENT, C_TRI, C_IOTA, C_HALVES, C_ODD, C_RANK, C_SEG = 0, 128, 256, 320, 384, 448, 456


def segments_of(tiles):
    if tiles >= 90:
        last = [25, 25, 23]
        return [tiles - sum(last)] + last
    return [tiles - tiles // 2, tiles // 2]


def capacity_of(tokens, experts):
    return max(1, -int(-CAPACITY_FACTOR * tokens // experts))


def layout_of(n, e, experts):
    tiles = -(-n // P)
    edge_tiles = -(-e // P)
    group = -(-edge_tiles // tiles)
    third = -(-group // 3)
    subs = [third, third, group - 2 * third]
    seg = segments_of(tiles)
    caps = [P * (t + 1) for t in seg]
    base = [0]
    for c in caps:
        base.append(base[-1] + (experts + 1) * c)
    columns = -(-(n + WIN) // WIN) * WIN
    fins = min(MOST_FINS, columns // (4 * P))
    return dict(tiles=tiles, aggregate=columns, fins=fins, group=group, subs=subs, seg=seg, caps=caps, base=base,
                columns=(tiles + 1) * group, ffn=[t + experts - 1 for t in seg])


def buffer_of(s, last):
    return 2 if s == last else min(s, 1)


def paces_of(products, iterations):
    for pattern in ([2, 3, 3], [3, 3, 3], [4, 4, 3], [4, 4, 4]):
        paces = [2] + [pattern[j % 3] for j in range(iterations - 1)]
        if sum(paces) >= products:
            return paces
    return paces


def steps_of(tiles, seg, ffn, per_step):
    steps = [dict(agg=0), dict(agg=1)]
    node = f = k0 = place = 0
    last = len(seg) - 1
    ends = [seg[0], sum(seg[:last]), tiles]
    products, paces = [], [0] * tiles

    def plan_products(s):
        end = k0 + ffn[s] - EXTRA
        for k in range(k0, end):
            first = [("turn", k)] if k == k0 else []
            ahead = k + 2 < end
            products.append(first + [("layer1", k)] + [("rows", k + 2), ("weights1", k + 2)] * ahead)
            products.append([("turn", k + 1)] * (k + 1 < end) + [("layer2", k)] + [("weights2", k + 2)] * ahead)

    def take(it, n, s):
        n = min(n, len(products))
        if n:
            it["ops"] = [(max(0, i - n + 3) if n > 1 else 0, kind, k, buffer_of(s, last))
                         for i in range(n) for kind, k in products[i]]
            del products[:n]

    def fins(it, ready):
        nonlocal f, place
        if f < ready:
            which = next(g for g in range(3) if f < ends[g])
            n = min(per_step, ends[which] - f)
            it.update(fin=f, fins=n, source=which, place=place)
            f += n
            place = 1 - place

    for s, t in enumerate(seg):
        for j in range(t):
            it = dict(node=node)
            if node + LAG < tiles:
                it["agg"] = node + LAG
            if node:
                it["rank"] = node - 1
            if j:
                take(it, paces[j - 1], s - 1)
            elif s:
                it["plan"] = s - 1
            if s and j == 1:
                it.update(slots=s - 1, loaded=True)
            steps.append(it)
            if s and not j:
                steps.append(dict(sched=s - 1))
                plan_products(s - 1)
                paces = paces_of(len(products), t - 1)
                k0 += ffn[s - 1]
            node += 1
        while products:
            steps.append({})
            take(steps[-1], 4, s - 1)
        if s:
            steps.append(dict(extra=s - 1))
    steps.append(dict(rank=tiles - 1, plan=last, slots=last))
    fins(steps[-1], ends[1])
    steps.append(dict(sched=last))
    plan_products(last)
    while products or f < ends[1]:
        it = {}
        take(it, 4, last)
        fins(it, ends[1])
        steps.append(it)
    steps += [dict(extra=last), dict(sched=len(seg))]
    while f < tiles:
        steps.append({})
        fins(steps[-1], tiles)
    steps.append({})
    before = None
    for it in steps:
        if "sched" not in it and "extra" not in it:
            if before:
                it.update(done=before["fin"], dones=before["fins"], where=before["place"])
            before = it if "fin" in it else None
    return steps


MOVING = ("agg", "node", "rank", "fin", "done")


def timeline_of(steps, tiles):
    def alone(i):
        it = steps[i]
        seen = [s for s in steps[:i]]
        new_place = "fin" in it and not any(
            "fin" in s and s["place"] == it["place"] and s["fins"] >= it["fins"] for s in seen)
        return ("sched" in it or "extra" in it or "plan" in it or "slots" in it or it.get("agg") in (0, tiles - 1) or it.get("node") in (0, tiles - 1)
                or it.get("rank") in (0, tiles - 1)
                or any(k < 2 for _, _, k, _ in it.get("ops", [])) or new_place
                or ("fin" in it and it["fin"] + it["fins"] == tiles)
                or ("done" in it and it["done"] + it["dones"] == tiles))

    def same(a, b, strides):
        ops, later_ops = a.get("ops", []), b.get("ops", [])
        return a.keys() == b.keys() and all(
            b[x] - a[x] == strides.setdefault(x, b[x] - a[x]) if x in MOVING else x == "ops" or a[x] == b[x]
            for x in a) and len(ops) == len(later_ops) and all(
            o[:2] + o[3:] == p[:2] + p[3:] and p[2] - o[2] == strides.setdefault("ffn", p[2] - o[2])
            for o, p in zip(ops, later_ops))

    out, i = [], 0
    while i < len(steps):
        best = (1, 1, {})
        for period in (1, 2, 3, 4):
            if i + 2 * period > len(steps) or any(alone(i + j) for j in range(period)):
                continue
            strides, count = {}, 1
            while i + (count + 1) * period <= len(steps) and not any(
                    alone(i + count * period + j) for j in range(period)) and all(
                    same(steps[i + (count - 1) * period + j], steps[i + count * period + j], strides)
                    for j in range(period)):
                count += 1
            if count > 1 and strides.get("ffn", 2) % 2 == 0 and count * period > best[0] * best[1]:
                best = (count, period, strides)
        count, period, strides = best
        out.append((count, steps[i:i + period], strides))
        i += count * period
    return out


def gnn_moe_kernel(nc, x, src_t, dst_t, w_t, w_gnn, b_gnn, gate_w, gate_b, w1, b1, w2, b2, consts, limits,
                   zeros, out, sizes):
    N, D = x.shape
    E8 = gate_w.shape[2]
    F = b1.shape[1] * b1.shape[2]
    FC = F // P
    KD = D // P
    HALF = FC // 2
    NT, G, SUBS, SEG, CAPS, BASE, COLS, FFN = (sizes[q] for q in (
        "tiles", "group", "subs", "seg", "caps", "base", "columns", "ffn"))
    OFF = [0, SUBS[0], SUBS[0] + SUBS[1]]
    NG = NT
    LAST_ROWS = N - (NT - 1) * P
    CAP = capacity_of(N, E8)
    NC, FINS = sizes["aggregate"], sizes["fins"]
    LATE_FINS = 2 * FINS
    WINDOWS = NC // WIN
    S = len(SEG)
    KTOT = sum(FFN)
    ROWS = BASE[-1]
    STEPS = steps_of(NT, SEG, FFN, FINS)
    TIMELINE = timeline_of(STEPS, NT)
    LN_ROWS = P * LN_TILES
    LN_FULL = N // LN_ROWS
    assert D == 2 * P and E8 == 8 and min(SEG) >= 7 and max(FFN) <= 48 and LAST_ROWS > 0

    ln_dram = nc.dram_tensor("normed", (N, D), F32).ap()
    x2_dram = nc.dram_tensor("x_after_gnn", (N, D), F32).ap()
    hbuf = nc.dram_tensor("rows_by_expert", (ROWS, D), F32).ap()
    KBUF = [0, FFN[0], sum(FFN[:-1]), KTOT]
    ybuf = [nc.dram_tensor(f"expert_outputs{g}", (max(KBUF[g + 1] - KBUF[g], 1) * P, D), F32).ap() for g in range(3)]

    with ExitStack() as ctx:
        def sb(name, shape, dt=F32):
            return ctx.enter_context(nc.sbuf_tensor(name, shape, dt))

        def psum(name, shape):
            return ctx.enter_context(nc.psum_tensor(name, shape, F32))

        def sem(name):
            return ctx.enter_context(nc.semaphore(name))

        aggT = sb("aggT", [P, KD, NC])
        src_sb = sb("src_sb", [P, COLS], I32)
        rel = sb("rel", [P, COLS])
        wgt = sb("wgt", [P, COLS])
        base_bc = sb("base_bc", [P, 3 * (NG + 1)])
        base_i = sb("base_i", [1, 3 * (NG + 1)], I32)
        msg = sb("msg", [P, G, D])
        onehot = sb("onehot", [P, G, WIN])
        idx = sb("idx", [P, G], I32)
        cst = sb("cst", [P, C_SEG + E8 * S])
        ones = sb("ones", [P, P])
        eps = sb("eps", [P, 1])
        wg_sb = sb("wg_sb", [P, KD, D])
        bg_sb = sb("bg_sb", [P, D])
        gw_sb = sb("gw_sb", [P, KD, E8])
        gb_sb = sb("gb_sb", [P, E8])
        aggS = sb("aggS", [P, KD, P])
        xt = sb("xt", [P, D])
        hrow = sb("hrow", [P, D])
        hTs = sb("hTs", [P, KD, P])
        st6 = sb("st6", [P, 6])
        mv = sb("mv", [P, 2])
        sd = sb("sd", [P, 1])
        rs = sb("rs", [P, 1])
        rt = sb("rt", [P, 8 * E8])
        sc = sb("sc", [P, 8])
        slot_i = sb("slot_i", [P, 1], I32)
        slots = sb("slots", [P, NT])
        chosen = sb("chosen", [P, NT])
        gain = sb("gain", [P, NT])
        seen = sb("seen", [P, E8])
        offs = sb("offs", [P, E8])
        WSZ = KD * F + FC * D + FC + D
        wsl = sb("wsl", [P, 2, WSZ])
        hin = sb("hin", [P, 2, D])
        hTf = sb("hTf", [P, KD, P])
        hmid = sb("hmid", [P, FC, P])
        yrow = sb("yrow", [P, 2, D])
        plan = sb("plan", [1, 4 * KTOT], I32)
        pads = sb("pads", [1, E8 * S], I32)
        more_i = sb("more_i", [1, S], I32)
        junk = sb("junk", [P, D])
        fix = sb("fix", [P, 2 * D])
        fix2 = sb("fix2", [P, D])
        yidx = sb("yidx", [P, LATE_FINS], I32)
        finite = sb("finite", [P, NT])
        flag_i = sb("flag_i", [1, 2], I32)
        flag_bc = sb("flag_bc", [P, 1])

        ps_agg = psum("ps_agg", [P, 2, 512])
        ps_x2 = psum("ps_x2", [P, 512])
        ps_tr = psum("ps_tr", [P, 512])
        ps_in = psum("ps_in", [P, 512])
        ps_h = psum("ps_h", [P, FC, P])
        ps_y = psum("ps_y", [P, 512])

        ident = cst[:, C_IDENT:C_IDENT + P]
        tri = cst[:, C_TRI:C_TRI + P]
        iota = cst[:, C_IOTA:C_IOTA + WIN]
        halves = cst[:, C_HALVES:C_HALVES + WIN]
        oddity = cst[:, C_ODD:C_ODD + WIN]
        rank8 = cst[:, C_RANK:C_RANK + E8]

        def w1_at(b):
            return wsl[:, b, 0:KD * F].rearrange("p (k f) -> p k f", k=KD)

        def w2_at(b):
            return wsl[:, b, KD * F:KD * F + FC * D].rearrange("p (c d) -> p c d", c=FC)

        def b1_at(b):
            return wsl[:, b, KD * F + FC * D:KD * F + FC * D + FC]

        def b2_at(b):
            return wsl[:, b, WSZ - D:WSZ]

        ln_space = wsl[:, :, :].rearrange("p a b -> p (a b)")

        def ln_buf(u):
            return ln_space[:, u * LN_TILES * D:(u + 1) * LN_TILES * D].rearrange("p (t d) -> p t d", d=D)

        agg_flat = aggT[:, :, :].rearrange("p k c -> p (k c)")

        def yg_at(place):
            return agg_flat[:, place * D:(place + 1) * D]

        def xg_at(place):
            return agg_flat[:, (LATE_FINS + place) * D:(LATE_FINS + place + 1) * D]

        ln_small = sb("ln_small", [P, LN_BUFS, LN_TILES, 10])
        msg_flat = msg[:, :, :].rearrange("p g d -> p (g d)")
        dst_i = msg_flat[:, 0:COLS].bitcast(I32)
        lim_sb = msg_flat[:, COLS:COLS + 3 * (NG + 1)]
        chk = msg_flat[:, COLS + 3 * (NG + 1):COLS + 6 * (NG + 1) + 8]

        s_const = sem("s_const")
        s_dst = sem("s_dst")
        s_edges = sem("s_edges")
        s_memset = sem("s_memset")
        s_lnx = [sem(f"s_lnx{u}") for u in range(LN_BUFS)]
        s_lnmv = sem("s_lnmv")
        s_lnsd = sem("s_lnsd")
        s_lnrs = sem("s_lnrs")
        s_lny = sem("s_lny")
        s_lnst = [sem(f"s_lnst{u}") for u in range(LN_BUFS)]
        s_lnc = sem("s_lnc")
        s_lnl = sem("s_lnl")
        s_pre = sem("s_pre")
        s_zero = sem("s_zero")
        s_prepe = sem("s_prepe")
        s_flag = sem("s_flag")
        g_idx, g_msg, g_onehot, g_mm, g_dve = (sem(q) for q in ("g_idx", "g_msg", "g_onehot", "g_mm", "g_dve"))
        s_idx = [sem(f"s_idx{q}") for q in range(3)]
        s_onehot = [sem(f"s_onehot{q}") for q in range(3)]
        s_msg = [sem(f"s_msg{q}") for q in range(3)]
        s_mm = [sem(f"s_mm{q}") for q in range(3)]
        s_added = [sem(f"s_added{q}") for q in range(3)]
        s_eq = sem("s_eq")
        s_aggS, s_n1, s_xt, s_x2, s_x2st = (sem(q) for q in ("s_aggS", "s_n1", "s_xt", "s_x2", "s_x2st"))
        s_nlink, s_mv, s_sd, s_h = (sem(q) for q in ("s_nlink", "s_mv", "s_sd", "s_h"))
        s_tr, s_hTs, s_log, s_ls, s_exp, s_choice, s_rank, s_route, s_scat = (
            sem(q) for q in ("s_tr", "s_hTs", "s_log", "s_ls", "s_exp", "s_choice", "s_rank", "s_route", "s_scat"))
        s_slink, s_slotlink, s_ends, s_plan, s_pad, s_dummy = (
            sem(q) for q in ("s_slink", "s_slotlink", "s_ends", "s_plan", "s_pad", "s_dummy"))
        s_hin = [sem(f"s_hin{b}") for b in range(2)]
        s_w1 = [sem(f"s_w1_{b}") for b in range(2)]
        s_w2 = [sem(f"s_w2_{b}") for b in range(2)]
        s_yst = [sem(f"s_yst{b}") for b in range(2)]
        s_ft, s_hTf, s_l1, s_relu, s_l2, s_y = (sem(q) for q in ("s_ft", "s_hTf", "s_l1", "s_relu", "s_l2", "s_y"))
        s_yidx, s_fin, s_checked = (sem(q) for q in ("s_yidx", "s_fin", "s_checked"))
        s_yg = [sem(f"s_yg{b}") for b in range(LATE_FINS)]
        s_xg = [sem(f"s_xg{b}") for b in range(LATE_FINS)]
        s_out = [sem(f"s_out{b}") for b in range(LATE_FINS)]
        s_redo, s_redope, s_again = (sem(q) for q in ("s_redo", "s_redope", "s_again"))
        r_idx, r_in, r_dve, r_out = (sem(q) for q in ("r_idx", "r_in", "r_dve", "r_out"))
        s_held = {q: sem("s_held_" + q) for q in ("sp", "act", "pe", "dve", "pool")}

        def finite_col(f, r):
            return finite[0:r, bass.ds(f, 1)]

        def known(value):
            return isinstance(value, int)

        def later(value):
            return not (known(value) and value == 0)

        def hold(eng, name, semaphore, value):
            eng.wait_ge(semaphore, value)
            if not known(value):
                eng.sem_inc(s_held[name], 1)

        class Links:

            def __init__(self, eng, name, semaphore, start):
                self.eng, self.name, self.semaphore, self.start, self.n = eng, name, semaphore, start, 0

            def mark(self, instruction):
                instruction.then_inc(self.semaphore, 1)
                self.n += 1

            def wait(self):
                hold(self.eng, self.name, self.semaphore, self.start + self.n)

            def __call__(self, instruction):
                self.mark(instruction)
                self.wait()

        @contextmanager
        def iterations(eng, count):
            if count == 1:
                yield 0
            else:
                with eng.Fori(0, count) as t:
                    yield t

        def walk(eng, steps, sched=None, extra=None):
            used = {kind: [0] * LATE_FINS for kind in ("fin", "done")}
            for count, body, strides in TIMELINE:
                if "sched" in body[0]:
                    if sched:
                        sched(body[0]["sched"])
                    continue
                if "extra" in body[0]:
                    if extra:
                        extra(body[0]["extra"])
                    continue
                where = [(kind, it[kind + "s"], FINS * it["place" if kind == "fin" else "where"])
                         for it in body for kind in used if kind in it]
                per_body = {kind: [sum(first <= p < first + n for k, n, first in where if k == kind)
                                   for p in range(LATE_FINS)] for kind in used}
                with iterations(eng, count) as t:
                    here = {kind: list(of) for kind, of in used.items()}
                    for it in body:
                        at = {x: it[x] + t * strides.get(x, 0) if x in it else None for x in MOVING}

                        def ops(slot, it=it, t=t):
                            return [(kind, k + t * strides.get("ffn", 0), k % 2, to)
                                    for where, kind, k, to in it.get("ops", []) if where == slot]

                        def last_stage(kind, key):
                            tiles = []
                            for j in range(it.get(kind + "s", 0)):
                                place = it[key] * FINS + j
                                tiles.append((at[kind] + j, place, here[kind][place] + t * per_body[kind][place]))
                                here[kind][place] += 1
                            return tiles

                        steps(at["agg"], at["node"], at["rank"], ops, last_stage("fin", "place"),
                              last_stage("done", "where"), it)
                for kind in used:
                    used[kind] = [u + n * count for u, n in zip(used[kind], per_body[kind])]

        def extra_tiles(s):
            end = sum(FFN[:s + 1])
            return [(k, k % 2) for k in range(end - EXTRA, end)]

        def if_needed(eng, s, work, skip):
            needed = eng.value_load(more_i[0:1, s:s + 1], min_val=0, max_val=1)
            with eng.If(needed >= 1):
                for k, b in extra_tiles(s):
                    work(k, b)
            with eng.Else():
                skip()

        def all_stored(eng):
            for place in range(LATE_FINS):
                n = sum(1 for it in STEPS for j in range(it.get("fins", 0)) if FINS * it["place"] + j == place)
                if n:
                    eng.wait_ge(s_out[place], 16 * n)
            eng.wait_ge(s_redo, 3)

        def each_row_tile(eng, step):
            step(0, P)
            with eng.Fori(1, NT - 1) as f:
                step(f, P)
            step(NT - 1, LAST_ROWS)

        def rows_of(n):
            return LAST_ROWS if known(n) and n == NT - 1 else P

        def of_parity(total, b):
            return (total + 1 - b) // 2

        def half(k, b):
            return (k - b) // 2

        def ln_stores(u):
            total = 16 * len([b for b in range(LN_FULL) if b % LN_BUFS == u])
            left = N - LN_FULL * LN_ROWS
            if u == LN_FULL % LN_BUFS:
                total += 16 * ((left // P > 0) + (left % P > 0))
            return total

        LN_TOTAL = LN_FULL + (N > LN_FULL * LN_ROWS)

        def ln_tiles(b):
            return LN_TILES if b < LN_FULL else -(-(N - LN_FULL * LN_ROWS) // P)

        def ln_rows(b, t):
            left = N - LN_FULL * LN_ROWS
            return left % P if known(b) and b == LN_FULL and t == left // P else P

        def ln_batches(eng, ahead, batch):
            total, tiles_of = LN_TOTAL, ln_tiles
            rounds = (total - 2) // LN_BUFS
            ahead(0, 0, tiles_of(0))
            if rounds > 0:
                with iterations(eng, rounds) as r:
                    for u in range(LN_BUFS):
                        ahead(r * LN_BUFS + u + 1, (u + 1) % LN_BUFS, LN_TILES)
                        batch(r * LN_BUFS + u, u, LN_TILES)
            for b in range(rounds * LN_BUFS, total):
                if b + 1 < total:
                    ahead(b + 1, (b + 1) % LN_BUFS, tiles_of(b + 1))
                batch(b, b % LN_BUFS, tiles_of(b))

        LINKS_NODE, LINKS_RANK, LINKS_PLAN, LINKS_SLOTS, LINKS_REDO = 19, 8, 37, 7, 7
        block = ctx.enter_context(nc.Block())

        @block.sync
        def _(sp):
            sp.dma_start(dst_i, dst_t).then_inc(s_dst, 16)

            def load(b, u, again):
                if again is not None:
                    hold(sp, "sp", s_lnst[u], again)
                sp.dma_start(ln_buf(u), x[bass.ds(b * LN_ROWS, LN_ROWS), :].rearrange(
                    "(p t) d -> p t d", t=LN_TILES)).then_inc(s_lnx[u], 16)

            rounds = LN_FULL // LN_BUFS
            if rounds:
                for u in range(LN_BUFS):
                    load(u, u, None)
            for dst, source in ((cst[:, :], consts), (wg_sb[:, :, :], w_gnn), (gw_sb[:, :, :], gate_w),
                                (bg_sb[:, :], b_gnn.partition_broadcast(P)),
                                (gb_sb[:, :], gate_b.partition_broadcast(P))):
                sp.dma_start(dst, source).then_inc(s_const, 16)
            for dst, source in ((src_sb[:, :], src_t), (wgt[:, :], w_t), (lim_sb, limits)):
                sp.dma_start(dst, source).then_inc(s_edges, 16)
            if rounds > 1:
                with sp.Fori(1, rounds) as r:
                    for u in range(LN_BUFS):
                        load(r * LN_BUFS + u, u, r * 16)
            for b in range(rounds * LN_BUFS, LN_FULL):
                load(b, b % LN_BUFS, 16 * (b // LN_BUFS))
            b, u = LN_FULL, LN_FULL % LN_BUFS
            left = N - LN_FULL * LN_ROWS
            if b >= LN_BUFS:
                hold(sp, "sp", s_lnst[u], 16 * (b // LN_BUFS))
            if left // P:
                sp.dma_start(ln_buf(u)[:, 0:left // P, :], x[b * LN_ROWS:b * LN_ROWS + left // P * P, :].rearrange(
                    "(p t) d -> p t d", t=left // P)).then_inc(s_lnx[u], 16)
            if left % P:
                sp.dma_start(ln_buf(u)[0:left % P, left // P, :], x[N - left % P:N, :]).then_inc(s_lnx[u], 16)
            for s in range(S):
                row = BASE[s] + E8 * CAPS[s]
                sp.dma_start(hbuf[row:row + P, :], zeros).then_inc(s_dummy, 16)
                to = buffer_of(s, S - 1)
                for k, _ in extra_tiles(s):
                    row = (k - KBUF[to]) * P
                    sp.dma_start(ybuf[to][row:row + P, :], zeros).then_inc(s_dummy, 16)
            for u in range(LN_BUFS):
                hold(sp, "sp", s_lnst[u], ln_stores(u))

            def rows(k, b):
                first = sp.snap(sp.value_load(plan[0:1, bass.ds(k * 4 + 1, 1)], min_val=0, max_val=ROWS - P))
                if not (known(k) and k < 2):
                    hold(sp, "sp", s_ft, k - 1)
                sp.dma_start(hin[:, b, :], hbuf[bass.ds(first, P), :]).then_inc(s_hin[b], 16)

            def weights(k, b, signal, used, pairs):
                expert = sp.value_load(plan[0:1, bass.ds(k * 4, 1)], min_val=0, max_val=E8 - 1)
                changed = sp.value_load(plan[0:1, bass.ds(k * 4 + 3, 1)], min_val=0, max_val=1)
                expert = sp.snap(expert)
                if not (known(k) and k < 2):
                    used()
                with sp.If(changed >= 1):
                    for dst, source in pairs:
                        sp.dma_start(dst, source[bass.ds(expert, 1)].rearrange(
                            "e p c d -> p (e c) d" if len(source.shape) == 4 else "e p d -> p (e d)")
                            ).then_inc(signal[b], 16)
                with sp.Else():
                    sp.sem_inc(signal[b], 32)

            def weights1(k, b):
                weights(k, b, s_w1, lambda: hold(sp, "sp", s_relu, k * 2 - 2), ((w1_at(b), w1), (b1_at(b), b1)))

            def weights2(k, b):
                weights(k, b, s_w2, lambda: hold(sp, "sp", s_y, k - 1), ((w2_at(b), w2), (b2_at(b), b2)))

            def experts_work(ops):
                for kind, k, b, to in ops:
                    if kind == "rows":
                        rows(k, b)
                    elif kind == "weights1":
                        weights1(k, b)
                    elif kind == "weights2":
                        weights2(k, b)

            def load_x(n):
                if later(n):
                    hold(sp, "sp", s_x2st, n * 16)
                    hold(sp, "sp", s_h, n)
                r = rows_of(n)
                sp.dma_start(xt[0:r, :], x[bass.ds(n * P, r), :]).then_inc(s_xt, 16)

            def steps(a, n, m, ops, fins, done, it):
                if n is not None and "loaded" not in it:
                    load_x(n)
                experts_work(ops(0))
                if n is not None:
                    r = rows_of(n)
                    hold(sp, "sp", s_x2, n + 1)
                    sp.dma_start(x2_dram[bass.ds(n * P, r), :], xt[0:r, :]).then_inc(s_x2st, 16)
                if fins and not later(fins[0][0]):
                    sp.wait_ge(s_x2st, 16 * NT)
                    sp.wait_ge(s_aggS, NT)
                for f, place, used in fins:
                    r = rows_of(f)
                    if later(used):
                        hold(sp, "sp", s_out[place], used * 16)
                    sp.dma_start(xg_at(place)[0:r, :], x2_dram[bass.ds(f * P, r), :]).then_inc(s_xg[place], 16)
                experts_work(ops(1))
                experts_work(ops(2))

            def sched(s):
                if s == S:
                    return
                k0, nodes = sum(FFN[:s]), sum(SEG[:s + 1])
                hold(sp, "sp", s_ends, s + 1)
                sp.wait_ge(s_scat, 16 * nodes)
                for e in range(E8):
                    row = sp.value_load(pads[0:1, s * E8 + e:s * E8 + e + 1], min_val=0, max_val=ROWS - P)
                    sp.dma_start(hbuf[bass.ds(row, P), :], zeros).then_inc(s_pad, 16)
                if s < S - 1:
                    load_x(nodes + 1)
                hold(sp, "sp", s_plan, s + 1)
                weights1(k0, k0 % 2)
                sp.wait_ge(s_pad, 16 * E8 * (s + 1))
                sp.wait_ge(s_dummy, 16 * (1 + EXTRA) * S)
                rows(k0, k0 % 2)
                rows(k0 + 1, (k0 + 1) % 2)
                weights2(k0, k0 % 2)
                weights1(k0 + 1, (k0 + 1) % 2)
                weights2(k0 + 1, (k0 + 1) % 2)

            def extra(s):
                def work(k, b):
                    rows(k, b)
                    weights1(k, b)
                    weights2(k, b)

                def skip():
                    for k, b in extra_tiles(s):
                        for signal, size in ((s_hin, 16), (s_w1, 32), (s_w2, 32)):
                            sp.wait_ge(signal[b], size * half(k, b))
                            sp.sem_inc(signal[b], size)

                if_needed(sp, s, work, skip)

            hold(sp, "sp", s_flag, 1)
            walk(sp, steps, sched, extra)
            all_stored(sp)
            redo = sp.value_load(flag_i[0:1, 1:2], min_val=0, max_val=1)
            with sp.If(redo >= 1):
                def again(f, r):
                    if later(f):
                        hold(sp, "sp", r_out, f * 16)
                    sp.dma_start(xg_at(1)[0:r, :], x2_dram[bass.ds(f * P, r), :]).then_inc(r_in, 16)
                    hold(sp, "sp", r_dve, f * LINKS_REDO + LINKS_REDO)
                    sp.dma_start(out[bass.ds(f * P, r), :], xg_at(1)[0:r, :]).then_inc(r_out, 16)

                each_row_tile(sp, again)
                sp.wait_ge(r_out, 16 * NT)
            with sp.Else():
                sp.sem_inc(s_held["sp"], 1)

        @block.gpsimd
        def _(pool):
            pool.memset(aggT[:, :, :], 0.0).then_inc(s_zero, 1)
            for u in range(LN_BUFS):
                pool.wait_ge(s_lnst[u], ln_stores(u))
            pool.wait_ge(s_flag, 1)
            fast = pool.value_load(flag_i[0:1, 0:1], min_val=0, max_val=1)
            with pool.If(fast < 1):
                with pool.Fori(0, NG) as g:
                    hold(pool, "pool", g_idx, g + 1)
                    for j in range(G):
                        pool.indirect_dma_start(
                            out=msg[:, j, :], out_offset=None, in_=ln_dram,
                            in_offset=bass.IndirectOffsetOnAxis(ap=idx[:, j:j + 1], axis=0)).then_inc(g_msg, 16)
            with pool.Else():
                pool.sem_inc(s_held["pool"], 1)

            def gather(a, q):
                hold(pool, "pool", s_idx[q], a + 1)
                for j in range(OFF[q], OFF[q] + SUBS[q]):
                    pool.indirect_dma_start(
                        out=msg[:, j, :], out_offset=None, in_=ln_dram,
                        in_offset=bass.IndirectOffsetOnAxis(ap=idx[:, j:j + 1], axis=0)).then_inc(s_msg[q], 16)

            def scatter(n):
                r = rows_of(n)
                hold(pool, "pool", s_route, n + 1)
                pool.indirect_dma_start(
                    out=hbuf, out_offset=bass.IndirectOffsetOnAxis(ap=slot_i[0:r, 0:1], axis=0),
                    in_=hrow[0:r, :], in_offset=None).then_inc(s_scat, 16)

            def steps(a, n, m, ops, fins, done, it):
                if a is not None:
                    if known(a) and a == 0:
                        gather(a, 0)
                    gather(a, 1)
                    gather(a, 2)
                if m is not None:
                    scatter(m)
                if fins and not later(fins[0][0]):
                    pool.wait_ge(s_aggS, NT)
                for f, place, used in fins:
                    r = rows_of(f)
                    hold(pool, "pool", s_yidx, f + 1)
                    if known(f):
                        outputs_of(1 if it["source"] == 0 else S if it["source"] == 2 else S - 1)
                    pool.indirect_dma_start(
                        out=yg_at(place)[0:r, :], out_offset=None, in_=ybuf[it["source"]],
                        in_offset=bass.IndirectOffsetOnAxis(ap=yidx[0:r, place:place + 1], axis=0)
                    ).then_inc(s_yg[place], 16)
                if a is not None and not (known(a) and a == NG - 1):
                    gather(a + 1, 0)

            def outputs_of(segments):
                for q in range(2):
                    pool.wait_ge(s_yst[q], 16 * of_parity(sum(FFN[:segments]), q))

            def sched(s):
                if s == S:
                    outputs_of(s)

            walk(pool, steps, sched)
            all_stored(pool)
            redo = pool.value_load(flag_i[0:1, 1:2], min_val=0, max_val=1)
            with pool.If(redo >= 1):
                bounds = [0, SEG[0], sum(SEG[:-1]), NT]
                for g in range(3):
                    def again(f, r):
                        hold(pool, "pool", r_idx, f + 1)
                        pool.indirect_dma_start(
                            out=yg_at(1)[0:r, :], out_offset=None, in_=ybuf[g],
                            in_offset=bass.IndirectOffsetOnAxis(ap=yidx[0:r, 0:1], axis=0)).then_inc(r_in, 16)

                    end = min(bounds[g + 1], NT - 1)
                    if bounds[g] < end:
                        with pool.Fori(bounds[g], end) as f:
                            again(f, P)
                    if g == 2:
                        again(NT - 1, LAST_ROWS)
            with pool.Else():
                pool.sem_inc(s_held["pool"], 1)

        @block.scalar
        def _(act):
            act.wait_ge(s_memset, 2)

            def deviation(b, u, tiles):
                small = ln_small[:, u, 0:tiles, :]
                hold(act, "act", s_lnmv, b + 1)
                nc.scalar.activation(small[:, :, 8], small[:, :, 7], ACT.Sqrt, bias=eps[:, 0:1]).then_inc(s_lnsd, 1)

            def normalize(b, u, tiles):
                small = ln_small[:, u, 0:tiles, :]
                hold(act, "act", s_lnrs, b + 1)
                for t in range(tiles):
                    r = ln_rows(b, t)
                    last = nc.scalar.activation(ln_buf(u)[0:r, t, :], ln_buf(u)[0:r, t, :], ACT.Identity,
                                                bias=small[0:r, t, 9:10], scale=small[0:r, t, 8:9])
                last.then_inc(s_lny, 1)
                hold(act, "act", s_lny, b + 1)
                if known(b) and b == LN_FULL:
                    left = N - LN_FULL * LN_ROWS
                    if left // P:
                        act.dma_start(ln_dram[b * LN_ROWS:b * LN_ROWS + left // P * P, :].rearrange(
                            "(p t) d -> p t d", t=left // P), ln_buf(u)[:, 0:left // P, :]).then_inc(s_lnst[u], 16)
                    if left % P:
                        act.dma_start(ln_dram[N - left % P:N, :], ln_buf(u)[0:left % P, left // P, :]
                                      ).then_inc(s_lnst[u], 16)
                else:
                    act.dma_start(ln_dram[bass.ds(b * LN_ROWS, LN_ROWS), :].rearrange(
                        "(p t) d -> p t d", t=LN_TILES), ln_buf(u)).then_inc(s_lnst[u], 16)

            ln_batches(act, deviation, normalize)

            def relu(k, b):
                hold(act, "act", s_w1[b], half(k, b) * 32 + 32)
                for c in range(FC):
                    if c % HALF == 0:
                        hold(act, "act", s_l1, k * 2 + c // HALF + 1)
                    ins = nc.scalar.activation(hmid[:, c, :], ps_h[:, c, :], ACT.Relu, bias=b1_at(b)[:, c:c + 1])
                    if c % HALF == HALF - 1:
                        ins.then_inc(s_relu, 1)

            def experts_work(ops, between=()):
                between = list(between)
                for kind, k, b, to in ops:
                    if kind == "layer1":
                        relu(k, b)
                        check(between[:2])
                        del between[:2]
                    elif kind == "layer2":
                        row = act.snap(act.value_load(plan[0:1, bass.ds(k * 4 + 2, 1)], min_val=0,
                                                      max_val=(KBUF[to + 1] - KBUF[to] - 1) * P))
                        hold(act, "act", s_y, k + 1)
                        act.dma_start(ybuf[to][bass.ds(row, P), :], yrow[:, b, :]).then_inc(s_yst[b], 16)
                check(between)

            def check(tiles):
                for f, place, used in tiles:
                    r = rows_of(f)
                    hold(act, "act", s_fin, f + 1)
                    nc.scalar.activation(junk[0:r, :], xg_at(place)[0:r, :], ACT.Copy, scale=0.0,
                                         accum_out=finite_col(f, r)).then_inc(s_checked, 1)
                    hold(act, "act", s_checked, f + 1)
                    act.dma_start(out[bass.ds(f * P, r), :], xg_at(place)[0:r, :]).then_inc(s_out[place], 16)

            def steps(a, n, m, ops, fins, done, it):
                if n is None and m is None:
                    experts_work(ops(0) + ops(1) + ops(2), done)
                    return
                if n is not None:
                    hold(act, "act", s_added[2], min(n + LAG, NG) if known(n) else n + LAG)
                    if later(n):
                        hold(act, "act", s_n1, n)
                    nc.scalar.copy(aggS[:, :, :], aggT[:, :, bass.ds(n * P, P)]).then_inc(s_aggS, 1)
                if m is not None:
                    hold(act, "act", s_ls, m + 1)
                    nc.scalar.activation(rt[:, 2 * E8:3 * E8], rt[:, E8:2 * E8], ACT.Exp,
                                         accum_out=sc[:, 1:2]).then_inc(s_exp, 1)
                experts_work(ops(0))
                if n is not None:
                    hold(act, "act", s_mv, n + 1)
                    nc.scalar.activation(sd[:, :], mv[:, 1:2], ACT.Sqrt, bias=eps[:, 0:1]).then_inc(s_sd, 1)
                experts_work(ops(1))
                if n is not None:
                    hold(act, "act", s_tr, n + 1)
                    if later(n):
                        hold(act, "act", s_log, n)
                    nc.scalar.copy(hTs[:, :, :], ps_tr[:, 0:D].rearrange("p (k t) -> p k t", k=KD)
                                   ).then_inc(s_hTs, 1)
                experts_work(ops(2))

            def extra(s):
                def skip():
                    act.wait_ge(s_relu, 2 * extra_tiles(s)[0][0])
                    act.sem_inc(s_relu, 2 * EXTRA)
                    for k, b in extra_tiles(s):
                        act.wait_ge(s_yst[b], 16 * half(k, b))
                        act.sem_inc(s_yst[b], 16)

                to = buffer_of(s, S - 1)
                if_needed(act, s, lambda k, b: experts_work([("layer1", k, b, to), ("layer2", k, b, to)]), skip)

            walk(act, steps, extra=extra)

        @block.tensor
        def _(pe):
            pe.wait_ge(s_memset, 2)
            pe.wait_ge(s_pre, 1)
            for q in range(3):
                firsts = rel[0:1, OFF[q]:OFF[q] + NG * G + 1:G]
                last = nc.tensor.matmul(ps_h[:, q, 0:NG + 1], ones[0:1, :], firsts, start=True, stop=True)
            last.then_inc(s_prepe, 1)
            pe.wait_ge(s_const, 80)
            pe.wait_ge(s_pre, 2)
            nc.tensor.transpose(ps_tr[0:1, 0:P], chk[:, 0:1], ident).then_inc(s_prepe, 1)
            pe.wait_ge(s_pre, 3)
            nc.tensor.matmul(ps_tr[:, P:P + 1], ones[0:1, :], chk[0:1, 2:3], start=True, stop=True
                             ).then_inc(s_prepe, 1)

            pe.wait_ge(s_flag, 1)
            fast = pe.value_load(flag_i[0:1, 0:1], min_val=0, max_val=1)
            with pe.If(fast < 1):
                with pe.Fori(0, NG) as g:
                    hold(pe, "pe", g_msg, g * (16 * G) + 16 * G)
                    with pe.Fori(0, WINDOWS) as w:
                        hold(pe, "pe", g_onehot, g * WINDOWS + w + 1)
                        for k in range(KD):
                            for j in range(G):
                                last = nc.tensor.matmul(ps_agg[:, 0, k * WIN:(k + 1) * WIN],
                                                        msg[:, j, k * P:(k + 1) * P], onehot[:, j, :],
                                                        start=j == 0, stop=j == G - 1)
                        last.then_inc(g_mm, 1)
            with pe.Else():
                pe.sem_inc(s_held["pe"], 1)

            def sub(a, q):
                hold(pe, "pe", s_msg[q], a * (16 * SUBS[q]) + 16 * SUBS[q])
                hold(pe, "pe", s_onehot[q], a + 1)
                if q == 2:
                    hold(pe, "pe", s_added[0], a + 1)
                elif later(a):
                    hold(pe, "pe", s_added[2 - q], a)
                for k in range(KD):
                    for j in range(OFF[q], OFF[q] + SUBS[q]):
                        last = nc.tensor.matmul(ps_agg[:, q % 2, k * WIN:(k + 1) * WIN],
                                                msg[:, j, k * P:(k + 1) * P], onehot[:, j, :],
                                                start=j == OFF[q], stop=j == OFF[q] + SUBS[q] - 1)
                last.then_inc(s_mm[q], 1)

            def gnn(n):
                hold(pe, "pe", s_aggS, n + 1)
                if later(n):
                    hold(pe, "pe", s_x2, n)
                for k in range(KD):
                    last = nc.tensor.matmul(ps_x2[:, 0:D], aggS[:, k, :], wg_sb[:, k, :],
                                            start=k == 0, stop=k == KD - 1)
                last.then_inc(s_n1, 1)

            def turn_node(n):
                hold(pe, "pe", s_h, n + 1)
                if later(n):
                    hold(pe, "pe", s_route, n)
                for k in range(KD):
                    last = nc.tensor.transpose(ps_tr[:, k * P:(k + 1) * P], hrow[:, k * P:(k + 1) * P], ident)
                last.then_inc(s_tr, 1)

            def logits(n):
                hold(pe, "pe", s_hTs, n + 1)
                for k in range(KD):
                    last = nc.tensor.matmul(ps_tr[:, D:D + E8], hTs[:, k, :], gw_sb[:, k, :],
                                            start=k == 0, stop=k == KD - 1)
                last.then_inc(s_log, 1)

            def ranks(n):
                r = rows_of(n)
                hold(pe, "pe", s_choice, n + 1)
                choice = rt[0:r, 3 * E8:4 * E8]
                nc.tensor.matmul(ps_tr[:, D + E8:D + 2 * E8], tri[0:r, :], choice, start=True, stop=True)
                nc.tensor.matmul(ps_tr[:, D + 2 * E8:D + 3 * E8], ones[0:r, :], choice, start=True, stop=True
                                 ).then_inc(s_rank, 1)

            def turn_ffn(k, b):
                hold(pe, "pe", s_hin[b], half(k, b) * 16 + 16)
                if not (known(k) and k == 0):
                    hold(pe, "pe", s_hTf, k)
                for q in range(KD):
                    last = nc.tensor.transpose(ps_in[:, q * P:(q + 1) * P], hin[:, b, q * P:(q + 1) * P], ident)
                last.then_inc(s_ft, 1)

            def layer1(k, b):
                hold(pe, "pe", s_hTf, k + 1)
                hold(pe, "pe", s_w1[b], half(k, b) * 32 + 32)
                for c in range(FC):
                    for q in range(KD):
                        last = nc.tensor.matmul(ps_h[:, c, :], w1_at(b)[:, q, c * P:(c + 1) * P], hTf[:, q, :],
                                                start=q == 0, stop=q == KD - 1)
                    if c % HALF == HALF - 1:
                        last.then_inc(s_l1, 1)

            def layer2(k, b):
                hold(pe, "pe", s_w2[b], half(k, b) * 32 + 32)
                if later(k):
                    hold(pe, "pe", s_y, k)
                for c in range(FC):
                    if c % HALF == 0:
                        hold(pe, "pe", s_relu, k * 2 + c // HALF + 1)
                    last = nc.tensor.matmul(ps_y[:, 0:D], hmid[:, c, :], w2_at(b)[:, c, :],
                                            start=c == 0, stop=c == FC - 1)
                last.then_inc(s_l2, 1)

            def experts_work(ops):
                for kind, k, b, to in ops:
                    if kind in ("turn", "layer1", "layer2"):
                        {"turn": turn_ffn, "layer1": layer1, "layer2": layer2}[kind](k, b)

            def steps(a, n, m, ops, fins, done, it):
                if a is not None:
                    sub(a, 0)
                if m is not None:
                    ranks(m)
                experts_work(ops(0))
                if n is not None:
                    gnn(n)
                if a is not None:
                    sub(a, 1)
                experts_work(ops(1))
                if a is not None:
                    sub(a, 2)
                if n is not None:
                    turn_node(n)
                experts_work(ops(2))
                if n is not None:
                    logits(n)

            def extra(s):
                def work(k, b):
                    turn_ffn(k, b)
                    layer1(k, b)
                    layer2(k, b)

                def skip():
                    before = extra_tiles(s)[0][0]
                    for signal, each in ((s_ft, 1), (s_l1, 2), (s_l2, 1)):
                        pe.wait_ge(signal, each * before)
                        pe.sem_inc(signal, each * EXTRA)

                if_needed(pe, s, work, skip)

            walk(pe, steps, extra=extra)
            pe.wait_ge(s_redo, 1)
            nc.tensor.transpose(ps_tr[0:1, 0:P], fix[:, 0:1], ident).then_inc(s_redope, 1)

        @block.vector
        def _(dve):
            dve.memset(ones[:, :], 1.0).then_inc(s_memset, 1)
            dve.memset(eps[:, :], EPS).then_inc(s_memset, 1)
            dve.wait_ge(s_memset, 2)

            def moments(b, u, tiles):
                small = ln_small[:, u, 0:tiles, :]
                hold(dve, "dve", s_lnx[u], ln_stores(u) if known(b) and b == LN_FULL
                     else b // LN_BUFS * 16 + 16 if known(b) else (b - u) * (16 // LN_BUFS) + 16)
                for t in range(tiles):
                    r = ln_rows(b, t)
                    last = dve.bn_stats(small[0:r, t, 0:6], ln_buf(u)[0:r, t, :])
                last.then_inc(s_lnc, 1)
                hold(dve, "dve", s_lnc, b + 1)
                for t in range(tiles):
                    r = ln_rows(b, t)
                    last = dve.bn_aggr(small[0:r, t, 6:8], small[0:r, t, 0:6])
                last.then_inc(s_lnmv, 1)

            def scales(b, u, tiles):
                link = Links(dve, "dve", s_lnl, b * 2)
                small = ln_small[:, u, 0:tiles, :]
                hold(dve, "dve", s_lnsd, b + 1)
                link(dve.reciprocal(small[:, :, 8], small[:, :, 8]))
                link(dve.scalar_tensor_tensor(out=small[:, :, 9], in0=small[:, :, 6], scalar=-1.0,
                                              in1=small[:, :, 8], op0=ALU.mult, op1=ALU.mult))
                dve.sem_inc(s_lnrs, 1)

            dve.memset(ln_small[:, :, :, :], 0.0).then_inc(s_memset, 1)
            dve.wait_ge(s_memset, 3)

            link = Links(dve, "dve", sem("s_prelink"), 0)
            dve.wait_ge(s_dst, 16)
            link(dve.tensor_copy(rel[:, :], dst_i))
            dve.sem_inc(s_pre, 1)
            dve.wait_ge(s_prepe, 1)
            firsts = base_bc[:, :].rearrange("p (g q) -> p g q", q=3)
            for q in range(3):
                link.mark(dve.tensor_copy(firsts[:, :, q], ps_h[:, q, 0:NG + 1]))
            link.wait()
            link.mark(dve.tensor_copy(base_i[0:1, :], base_bc[0:1, :]))
            rel3 = rel[:, :].rearrange("p (g j) -> p g j", j=G)
            for q in range(3):
                part = rel3[:, :, OFF[q]:OFF[q] + SUBS[q]]
                link.mark(dve.tensor_tensor(part, part, firsts[:, :, q:q + 1].to_broadcast([P, NG + 1, SUBS[q]]),
                                            ALU.subtract))

            def first_moments(b, u, tiles):
                if known(b) and b == 0:
                    moments(b, u, tiles)

            def scales_and_next(b, u, tiles):
                scales(b, u, tiles)
                if known(b):
                    if b < LN_TOTAL - 1:
                        moments(b + 1, (u + 1) % LN_BUFS, ln_tiles(b + 1))
                else:
                    moments(b + 1, (u + 1) % LN_BUFS, LN_TILES)

            ln_batches(dve, first_moments, scales_and_next)

            dve.wait_ge(s_const, 80)
            dve.wait_ge(s_edges, 48)
            link(dve.tensor_tensor(chk[:, 8:8 + 3 * (NG + 1)], base_bc[:, :], lim_sb, ALU.subtract))
            link.mark(dve.tensor_reduce(chk[:, 3:4], rel[:, :], AX_X, ALU.min))
            link.mark(dve.tensor_reduce(chk[:, 4:5], rel[:, :], AX_X, ALU.max))
            link(dve.tensor_reduce(chk[:, 5:6], chk[:, 8:8 + 3 * (NG + 1)], AX_X, ALU.min))
            link(dve.tensor_scalar(chk[:, 4:5], chk[:, 4:5], -1.0, float(WIN - 1), ALU.mult, ALU.add))
            link(dve.tensor_tensor(chk[:, 3:4], chk[:, 3:4], chk[:, 4:5], ALU.min))
            link(dve.tensor_tensor(chk[:, 0:1], chk[:, 3:4], chk[:, 5:6], ALU.min))
            dve.sem_inc(s_pre, 1)
            dve.wait_ge(s_prepe, 2)
            link(dve.tensor_reduce(chk[0:1, 1:2], ps_tr[0:1, 0:P], AX_X, ALU.min))
            link(dve.tensor_scalar(chk[0:1, 2:3], chk[0:1, 1:2], 0.0, None, ALU.is_ge))
            dve.sem_inc(s_pre, 1)
            link.mark(dve.tensor_copy(flag_i[0:1, 0:1], chk[0:1, 2:3]))
            dve.wait_ge(s_prepe, 3)
            link.mark(dve.tensor_copy(flag_bc[:, :], ps_tr[:, P:P + 1]))
            link.mark(dve.memset(seen[:, :], 0.0))
            link.mark(dve.memset(hrow[:, :], 0.0))
            link.mark(dve.memset(xt[:, :], 0.0))
            link.mark(dve.tensor_copy(offs[:, :], cst[:, C_SEG:C_SEG + E8]))
            link.mark(dve.memset(finite[:, :], 0.0))
            link.wait()
            dve.sem_inc(s_flag, 1)
            dve.wait_ge(s_zero, 1)

            fast = dve.value_load(flag_i[0:1, 0:1], min_val=0, max_val=1)
            with dve.If(fast < 1):
                at = fix[:, 0:G]
                with dve.Fori(0, NG) as g:
                    glink = Links(dve, "dve", g_dve, g * (5 + 4 * WINDOWS))
                    glink(dve.tensor_copy(idx[:, :], src_sb[:, bass.ds(g * G, G)]))
                    dve.sem_inc(g_idx, 1)
                    for q in range(3):
                        glink.mark(dve.tensor_tensor(
                            at[:, OFF[q]:OFF[q] + SUBS[q]], rel[:, bass.ds(g * G + OFF[q], SUBS[q])],
                            base_bc[:, bass.ds(g * 3 + q, 1)].to_broadcast([P, SUBS[q]]), ALU.add))
                    glink(dve.tensor_copy(fix[:, 32:32 + G], wgt[:, bass.ds(g * G, G)]))
                    with dve.Fori(0, WINDOWS) as w:
                        wlink = Links(dve, "dve", g_dve, g * (5 + 4 * WINDOWS) + w * 4 + 5)
                        wlink(dve.tensor_tensor(
                            onehot[:, :, :], iota.unsqueeze(1).to_broadcast([P, G, WIN]),
                            at.unsqueeze(2).to_broadcast([P, G, WIN]), ALU.is_equal))
                        wlink(dve.tensor_tensor(
                            onehot[:, :, :], onehot[:, :, :],
                            fix[:, 32:32 + G].unsqueeze(2).to_broadcast([P, G, WIN]), ALU.mult))
                        dve.sem_inc(g_onehot, 1)
                        hold(dve, "dve", g_mm, g * WINDOWS + w + 1)
                        columns = aggT[:, :, bass.ds(w * WIN, WIN)]
                        wlink(dve.tensor_tensor(
                            columns, columns, ps_agg[:, 0, 0:KD * WIN].rearrange("p (k c) -> p k c", k=KD), ALU.add))
                        wlink(dve.tensor_scalar(at, at, -float(WIN), None, ALU.add))
            with dve.Else():
                dve.sem_inc(s_held["dve"], 1)
            dve.tensor_scalar(wgt[:, :], wgt[:, :], flag_bc[:, 0:1], None, ALU.mult).then_inc(s_flag, 1)
            dve.wait_ge(s_flag, 2)

            def prep(a, q):
                n = SUBS[q]
                col = a * G + OFF[q]
                dve.tensor_copy(idx[:, OFF[q]:OFF[q] + n], src_sb[:, bass.ds(col, n)]).then_inc(s_idx[q], 1)
                hot = onehot[:, OFF[q]:OFF[q] + n, :]
                dve.tensor_tensor(hot, iota.unsqueeze(1).to_broadcast([P, n, WIN]),
                                  rel[:, bass.ds(col, n)].unsqueeze(2).to_broadcast([P, n, WIN]), ALU.is_equal
                                  ).then_inc(s_eq, 1)
                hold(dve, "dve", s_eq, a * 3 + q + 1)
                dve.tensor_tensor(hot, hot, wgt[:, bass.ds(col, n)].unsqueeze(2).to_broadcast([P, n, WIN]),
                                  ALU.mult).then_inc(s_onehot[q], 1)

            def sub(a, q):
                first = dve.snap(dve.value_load(base_i[0:1, bass.ds(a * 3 + q, 1)], min_val=0, max_val=N - 1))
                hold(dve, "dve", s_mm[q], a + 1)
                prev, val = (2, a) if q == 0 else (q - 1, a + 1)
                if not (known(a) and a == 0 and q == 0):
                    hold(dve, "dve", s_added[prev], val)
                columns = aggT[:, :, bass.ds(first, WIN)]
                dve.tensor_tensor(columns, columns, ps_agg[:, q % 2, 0:KD * WIN].rearrange("p (k c) -> p k c", k=KD), ALU.add
                                  ).then_inc(s_added[q], 1)
                prep(a + 1, q)

            def bias(n, link):
                hold(dve, "dve", s_xt, n * 16 + 16)
                link(dve.tensor_tensor(xt[:, :], xt[:, :], bg_sb[:, :], ALU.add))

            def norm_a(n, link):
                hold(dve, "dve", s_n1, n + 1)
                link.mark(dve.tensor_tensor(xt[:, :], xt[:, :], ps_x2[:, 0:D], ALU.add))
                link.wait()
                dve.sem_inc(s_x2, 1)
                link(dve.bn_stats(st6[:, :], xt[:, :]))
                link(dve.bn_aggr(mv[:, :], st6[:, :]))
                dve.sem_inc(s_mv, 1)

            def norm_b(n, link):
                hold(dve, "dve", s_sd, n + 1)
                link(dve.reciprocal(rs[:, :], sd[:, :]))
                if later(n):
                    hold(dve, "dve", s_scat, n * 16)
                dve.tensor_scalar(hrow[:, :], xt[:, :], mv[:, 0:1], rs[:, 0:1], ALU.subtract, ALU.mult
                                  ).then_inc(s_h, 1)

            def cols8(j):
                return rt[:, j * E8:(j + 1) * E8]

            def route_a(n, link):
                hold(dve, "dve", s_log, n + 1)
                link(dve.tensor_tensor(cols8(0), ps_tr[:, D:D + E8], gb_sb[:, :], ALU.add))
                link(dve.tensor_reduce(sc[:, 0:1], cols8(0), AX_X, ALU.max))
                link.mark(dve.tensor_scalar(cols8(1), cols8(0), sc[:, 0:1], None, ALU.subtract))
                link(dve.scalar_tensor_tensor(out=cols8(4), in0=cols8(0), scalar=sc[:, 0:1], in1=rank8,
                                              op0=ALU.is_ge, op1=ALU.mult))
                dve.sem_inc(s_ls, 1)
                link(dve.tensor_reduce(sc[:, 2:3], cols8(4), AX_X, ALU.max))
                link(dve.tensor_scalar(cols8(3), rank8, sc[:, 2:3], None, ALU.is_equal))
                dve.sem_inc(s_choice, 1)

            def route_b(n, link):
                hold(dve, "dve", s_rank, n + 1)
                hold(dve, "dve", s_exp, n + 1)
                link(dve.tensor_tensor(cols8(5), ps_tr[:, D + E8:D + 2 * E8], seen[:, :], ALU.add))
                link.mark(dve.tensor_tensor(seen[:, :], seen[:, :], ps_tr[:, D + 2 * E8:D + 3 * E8], ALU.add))
                link.mark(dve.tensor_tensor(cols8(6), cols8(5), cols8(3), ALU.mult))
                link.mark(dve.reciprocal(sc[:, 3:4], sc[:, 1:2]))
                link(dve.tensor_tensor(cols8(5), cols8(5), offs[:, :], ALU.add))
                link.mark(dve.tensor_reduce(sc[:, 4:5], cols8(6), AX_X, ALU.add))
                link(dve.tensor_tensor(cols8(7), cols8(5), cols8(3), ALU.mult))
                link(dve.tensor_reduce(sc[:, 5:6], cols8(7), AX_X, ALU.add))
                dve.scalar_tensor_tensor(out=gain[:, bass.ds(n, 1)], in0=sc[:, 4:5], scalar=float(CAP),
                                         in1=sc[:, 3:4], op0=ALU.is_lt, op1=ALU.mult)
                dve.tensor_copy(slots[:, bass.ds(n, 1)], sc[:, 5:6])
                dve.tensor_copy(chosen[:, bass.ds(n, 1)], sc[:, 2:3])
                dve.tensor_copy(slot_i[:, :], sc[:, 5:6]).then_inc(s_route, 1)
                assert link.n == LINKS_RANK, link.n

            def copy_in(k, b):
                hold(dve, "dve", s_ft, k + 1)
                if not (known(k) and k == 0):
                    hold(dve, "dve", s_l1, k * 2)
                dve.tensor_copy(hTf[:, :, :], ps_in[:, 0:D].rearrange("p (k t) -> p k t", k=KD)).then_inc(s_hTf, 1)

            def expert_out(k, b):
                hold(dve, "dve", s_w2[b], half(k, b) * 32 + 32)
                hold(dve, "dve", s_l2, k + 1)
                if not (known(k) and k < 2):
                    hold(dve, "dve", s_yst[b], half(k, b) * 16)
                dve.tensor_tensor(yrow[:, b, :], ps_y[:, 0:D], b2_at(b), ALU.add).then_inc(s_y, 1)

            def final_index(f, place, used):
                if later(used):
                    hold(dve, "dve", s_yg[place], used * 16)
                dve.tensor_copy(yidx[:, place:place + 1], slots[:, bass.ds(f, 1)]).then_inc(s_yidx, 1)

            def final(f, place, used):
                r = rows_of(f)
                hold(dve, "dve", s_yg[place], used * 16 + 16)
                hold(dve, "dve", s_xg[place], used * 16 + 16)
                dve.scalar_tensor_tensor(out=xg_at(place)[0:r, :], in0=yg_at(place)[0:r, :],
                                         scalar=gain[0:r, bass.ds(f, 1)], in1=xg_at(place)[0:r, :],
                                         op0=ALU.mult, op1=ALU.add).then_inc(s_fin, 1)

            def experts_work(ops):
                for kind, k, b, to in ops:
                    if kind == "turn":
                        copy_in(k, b)
                    elif kind == "layer2":
                        expert_out(k, b)

            def steps(a, n, m, ops, fins, done, it):
                link = Links(dve, "dve", s_nlink, n * LINKS_NODE) if n is not None else None
                pieces = planning(it["plan"]) if "plan" in it else iter(())
                for fin in fins:
                    final_index(*fin)
                for tile in done:
                    final(*tile)
                if a is not None:
                    sub(a, 0)
                if m is not None:
                    route_b(m, Links(dve, "dve", s_nlink, m * LINKS_NODE + LINKS_NODE - LINKS_RANK))
                if n is not None:
                    bias(n, link)
                next(pieces, None)
                experts_work(ops(0))
                if n is not None:
                    norm_a(n, link)
                if a is not None:
                    sub(a, 1)
                next(pieces, None)
                experts_work(ops(1))
                if n is not None:
                    norm_b(n, link)
                if a is not None:
                    sub(a, 2)
                for _ in pieces:
                    pass
                if "slots" in it:
                    point_to_outputs(it["slots"])
                experts_work(ops(2))
                if n is not None:
                    route_a(n, link)
                    assert link.n == LINKS_NODE - LINKS_RANK, link.n

            def planning(s):
                T, K, k0 = SEG[s], FFN[s], sum(FFN[:s])
                link = Links(dve, "dve", s_slink, s * LINKS_PLAN)
                io = iota[:, :]
                rows, n8, nt, cum, shift = (fix2[:, j * 8:(j + 1) * 8] for j in range(5))
                turns, mid = fix2[:, 40:41], fix2[:, 41:42]
                ek, stk, at, odd = (fix2[:, 48 + j * 48:48 + j * 48 + K] for j in range(4))
                segrow = cst[:, C_SEG + s * E8:C_SEG + (s + 1) * E8]
                dve.wait_ge(s_route, sum(SEG[:s + 1]))
                link(dve.tensor_tensor(rows, seen[:, :], offs[:, :], ALU.add))
                link(dve.tensor_copy(pads[0:1, s * E8:(s + 1) * E8], rows[0:1, :]))
                dve.sem_inc(s_ends, 1)
                link(dve.tensor_tensor(n8, rows, segrow, ALU.subtract))
                link(dve.tensor_scalar(n8, n8, 1.0 / P, None, ALU.mult))
                cmp = fix[:, 0:E8 * (T + 1)].rearrange("p (e q) -> p e q", e=E8)
                link(dve.tensor_tensor(cmp, io[:, 0:T + 1].unsqueeze(1).to_broadcast([P, E8, T + 1]),
                                       n8.unsqueeze(2).to_broadcast([P, E8, T + 1]), ALU.is_lt))
                link(dve.tensor_reduce(nt, cmp, AX_X, ALU.add))
                link(dve.tensor_copy(cum, nt))
                for e in range(1, E8):
                    link(dve.tensor_tensor(cum[:, e:e + 1], cum[:, e:e + 1], cum[:, e - 1:e], ALU.add))
                yield
                half_tiles = fix[:, 0:WIN]
                link(dve.tensor_scalar(half_tiles, io, 2.0, cum[:, E8 - 1:E8], ALU.mult, ALU.is_lt))
                link(dve.tensor_reduce(mid, half_tiles, AX_X, ALU.add))
                link(dve.tensor_scalar(turns, mid, 2.0, None, ALU.mult))
                link.mark(dve.tensor_scalar(more_i[0:1, s:s + 1], turns[0:1, :], float(K - EXTRA + 1), None, ALU.is_ge))
                link(dve.tensor_scalar(odd, oddity[:, 0:K], mid, None, ALU.mult))
                link(dve.tensor_tensor(at, halves[:, 0:K], odd, ALU.add))
                link(dve.tensor_tensor(at, at, io[:, 0:K], ALU.subtract))
                link(dve.scalar_tensor_tensor(out=at, in0=io[:, 0:K], scalar=turns, in1=at,
                                              op0=ALU.is_lt, op1=ALU.mult))
                link(dve.tensor_tensor(at, at, io[:, 0:K], ALU.add))
                past = fix[:, 0:K * E8].rearrange("p (k e) -> p k e", e=E8)
                link(dve.tensor_tensor(past, cum.unsqueeze(1).to_broadcast([P, K, E8]),
                                       at.unsqueeze(2).to_broadcast([P, K, E8]), ALU.is_le))
                link(dve.tensor_reduce(ek, past, AX_X, ALU.add))
                link(dve.tensor_tensor(past, past, nt.unsqueeze(1).to_broadcast([P, K, E8]), ALU.mult))
                link(dve.tensor_reduce(stk, past, AX_X, ALU.add))
                link(dve.tensor_tensor(stk, at, stk, ALU.subtract))
                link(dve.tensor_scalar(stk, stk, float(P), float(BASE[s]), ALU.mult, ALU.add))
                link(dve.scalar_tensor_tensor(out=stk, in0=ek, scalar=float(CAPS[s]), in1=stk,
                                              op0=ALU.mult, op1=ALU.add))
                rows4 = plan[0:1, 4 * k0:4 * (k0 + K)].rearrange("p (k c) -> p k c", c=4)
                link.mark(dve.tensor_scalar(rows4[:, :, 1], stk[0:1, :], float(BASE[s] + E8 * CAPS[s]), None, ALU.min))
                link.mark(dve.tensor_scalar(rows4[:, :, 2], at[0:1, :], float(P),
                                            float(P * (k0 - KBUF[buffer_of(s, S - 1)])), ALU.mult, ALU.add))
                link(dve.tensor_scalar(rows4[:, :, 0], ek[0:1, :], float(E8 - 1), None, ALU.min))
                link(dve.tensor_tensor(odd[0:1, 2:K], ek[0:1, 2:K], ek[0:1, 0:K - 2], ALU.not_equal))
                link.mark(dve.memset(rows4[:, 0:2, 3], 1))
                link(dve.scalar_tensor_tensor(out=rows4[:, 2:K, 3], in0=ek[0:1, 2:K], scalar=float(E8),
                                              in1=odd[0:1, 2:K], op0=ALU.is_lt, op1=ALU.mult))
                dve.sem_inc(s_plan, 1)
                if s + 1 < S:
                    yield
                    link(dve.tensor_tensor(offs[:, :], cst[:, C_SEG + (s + 1) * E8:C_SEG + (s + 2) * E8],
                                           seen[:, :], ALU.subtract))
                assert link.n == LINKS_PLAN - (s == S - 1), link.n

            def point_to_outputs(s):
                link = Links(dve, "dve", s_slotlink, s * LINKS_SLOTS)
                nt, cum, shift = (fix2[:, j * 8:(j + 1) * 8] for j in range(2, 5))
                segrow = cst[:, C_SEG + s * E8:C_SEG + (s + 1) * E8]
                link(dve.tensor_tensor(shift, cum, nt, ALU.subtract))
                link(dve.tensor_scalar(shift, shift, float(P),
                                       float(P * (sum(FFN[:s]) - KBUF[buffer_of(s, S - 1)])), ALU.mult, ALU.add))
                link(dve.tensor_tensor(shift, shift, segrow, ALU.subtract))
                n0, T = sum(SEG[:s]), SEG[s]
                part, step = slots[:, n0:n0 + T], fix2[:, 48:48 + T]
                mine = fix[:, 0:T * E8].rearrange("p (t e) -> p t e", e=E8)
                link(dve.tensor_tensor(mine, chosen[:, n0:n0 + T].unsqueeze(2).to_broadcast([P, T, E8]),
                                       rank8.unsqueeze(1).to_broadcast([P, T, E8]), ALU.is_equal))
                link(dve.tensor_tensor(mine, mine, shift.unsqueeze(1).to_broadcast([P, T, E8]), ALU.mult))
                link(dve.tensor_reduce(step, mine, AX_X, ALU.add))
                link(dve.tensor_tensor(part, part, step, ALU.add))
                assert link.n == LINKS_SLOTS, link.n

            for q in range(3):
                prep(0, q)

            def extra(s):
                def work(k, b):
                    copy_in(k, b)
                    expert_out(k, b)

                def skip():
                    for signal in (s_hTf, s_y):
                        dve.wait_ge(signal, extra_tiles(s)[0][0])
                        dve.sem_inc(signal, EXTRA)

                if_needed(dve, s, work, skip)

            walk(dve, steps, extra=extra)

            dve.wait_ge(s_checked, NT)
            end = Links(dve, "dve", s_again, 0)
            end(dve.tensor_scalar(fix[:, 32:32 + NT], finite[:, :], 0.0, None, ALU.is_equal))
            end(dve.tensor_reduce(fix[:, 0:1], fix[:, 32:32 + NT], AX_X, ALU.min))
            dve.sem_inc(s_redo, 1)
            dve.wait_ge(s_redope, 1)
            end(dve.tensor_reduce(fix[0:1, 1:2], ps_tr[0:1, 0:P], AX_X, ALU.min))
            end(dve.tensor_scalar(flag_i[0:1, 1:2], fix[0:1, 1:2], 1.0, None, ALU.is_lt))
            dve.sem_inc(s_redo, 2)
            all_stored(dve)
            redo = dve.value_load(flag_i[0:1, 1:2], min_val=0, max_val=1)
            with dve.If(redo >= 1):
                def again(f, r):
                    fix_link = Links(dve, "dve", r_dve, f * LINKS_REDO)
                    y, x2 = yg_at(1)[0:r, :], xg_at(1)[0:r, :]
                    kept, low, high = (msg[0:r, 1 + q, :] for q in range(3))
                    dve.tensor_copy(yidx[:, 0:1], slots[:, bass.ds(f, 1)]).then_inc(r_idx, 1)
                    hold(dve, "dve", r_in, f * 32 + 32)
                    fix_link(dve.tensor_scalar(y, y, gain[0:r, bass.ds(f, 1)], None, ALU.mult))
                    fix_link.mark(dve.tensor_scalar(low, y, -FLT_MAX, -1e4, ALU.is_lt, ALU.mult))
                    fix_link.mark(dve.tensor_scalar(kept.bitcast(I32), y, 0.0, 0.0, ALU.mult, ALU.is_equal))
                    fix_link(dve.tensor_scalar(high, y, FLT_MAX, 1e4, ALU.is_gt, ALU.mult))
                    fix_link(dve.tensor_tensor(low, low, high, ALU.add))
                    fix_link(dve.copy_predicated(low, kept.bitcast(I32), y))
                    fix_link(dve.tensor_tensor(x2, x2, low, ALU.add))
                    assert fix_link.n == LINKS_REDO

                each_row_tile(dve, again)
            with dve.Else():
                dve.sem_inc(s_held["dve"], 1)


def kernel(**inputs):
    import numpy as np
    import concourse.bacc as bacc
    from concourse.bass_utils import run_bass_kernel_spmd

    x = np.ascontiguousarray(inputs["x"])
    N, D = x.shape
    edges = inputs["src"].shape[0]
    experts = inputs["L0_ffn_gate_w"].shape[1]
    F = inputs["L0_ffn_b1"].shape[1]
    z = layout_of(N, edges, experts)
    NT, COLS, S = z["tiles"], z["columns"], len(z["seg"])

    def by_tile(a, fill):
        a = np.asarray(a)
        whole = np.full(COLS * P, fill, a.dtype)
        whole[:edges] = a
        return np.ascontiguousarray(whole.reshape(COLS, P).T)

    consts = np.zeros((P, C_SEG + experts * S), np.float32)
    consts[:, C_IDENT:C_IDENT + P] = np.eye(P)
    consts[:, C_TRI:C_TRI + P] = np.triu(np.ones((P, P)), 1)
    consts[:, C_IOTA:C_IOTA + WIN] = np.arange(WIN)
    consts[:, C_HALVES:C_HALVES + WIN] = np.arange(WIN) // 2
    consts[:, C_ODD:C_ODD + WIN] = np.arange(WIN) % 2
    consts[:, C_RANK:C_RANK + experts] = experts - np.arange(experts)
    for s in range(S):
        consts[:, C_SEG + s * experts:C_SEG + (s + 1) * experts] = z["base"][s] + z["caps"][s] * np.arange(experts)
    limits = np.broadcast_to(np.repeat(P * (np.arange(NT + 1) - 1), 3).astype(np.float32), (P, 3 * (NT + 1)))

    def rows(a, chunk):
        a = np.asarray(a)
        *lead, r, c = a.shape
        return np.ascontiguousarray(np.moveaxis(a.reshape(*lead, r // P, P, c), -3, -2))

    arrays = dict(
        x=x, src_t=by_tile(inputs["src"], 0), dst_t=by_tile(inputs["dst"], N - 1),
        w_t=by_tile(inputs["edge_weight"], 0),
        w_gnn=rows(np.asarray(inputs["L0_gnn_W"]).T, P), b_gnn=np.asarray(inputs["L0_gnn_b"]).reshape(1, D),
        gate_w=rows(inputs["L0_ffn_gate_w"], P), gate_b=np.asarray(inputs["L0_ffn_gate_b"]),
        w1=rows(inputs["L0_ffn_w1"], P),
        b1=np.ascontiguousarray(np.asarray(inputs["L0_ffn_b1"]).reshape(experts, F // P, P).transpose(0, 2, 1)),
        w2=rows(inputs["L0_ffn_w2"], P),
        b2=np.ascontiguousarray(np.broadcast_to(np.asarray(inputs["L0_ffn_b2"])[:, None, :], (experts, P, D))),
        consts=consts, limits=np.ascontiguousarray(limits), zeros=np.zeros((P, D), np.float32),
    )
    nc = bacc.Bacc("TRN2", target_bir_lowering=False, num_devices=1)
    args = {name: nc.dram_tensor(f"in_{name}", a.shape, mybir.dt.from_np(a.dtype), kind="ExternalInput").ap()
            for name, a in arrays.items()}
    out = nc.dram_tensor("out_x", (N, D), F32, kind="ExternalOutput").ap()
    gnn_moe_kernel(nc, *args.values(), out, z)
    r = run_bass_kernel_spmd(nc, [{f"in_{name}": a for name, a in arrays.items()}], core_ids=[0])
    return r.results[0]["out_x"]
```
